# Optimizing a Trainium2 kernel written in Bass

```python
import numpy as np
import jax
import jax.numpy as jnp

def _softmax(x, axis=-1):
    return jax.nn.softmax(x, axis=axis)

def _gelu(x):
    return jax.nn.gelu(x, approximate=True)

def _silu(x):
    return jax.nn.silu(x)

def _sigmoid(x):
    return jax.nn.sigmoid(x)

def _layernorm(x, axis=-1, eps=1e-05):
    m = jnp.mean(x, axis=axis, keepdims=True)
    v = jnp.var(x, axis=axis, keepdims=True)
    return (x - m) / jnp.sqrt(v + eps)

def _scatter_add(tgt, idx, src, axis=0):
    return tgt.at[idx].add(src)

def _segment_sum(src, seg, n):
    return jax.ops.segment_sum(src, seg, n)
kernel_name = 'mk_xattn_ffn_d1_seqx_r8_13922f'

def setup_inputs(seed: int=0):
    np.random.seed(seed)
    _w = jnp.asarray

    def _rec_inputs():
        import jax
        import jax.numpy as jnp
        _rk = jax.random.key(seed)
        x = 7.22e-05 + 1 * jax.random.normal(jax.random.fold_in(_rk, 1), (32, 128, 128), jnp.float32)
        _lenS = 128 - jax.random.randint(jax.random.fold_in(_rk, 7), (32,), 0, max(1, 128 // 4) + 1, jnp.int32)
        _lenS2 = 128 - jax.random.randint(jax.random.fold_in(_rk, 8), (32,), 0, max(1, 128 // 4) + 1, jnp.int32)
        _ctx_1024P = jax.random.normal(jax.random.fold_in(_rk, 11), (32, 16, 128), jnp.float32)
        _ctx_1024c = jax.random.dirichlet(jax.random.fold_in(_rk, 511), 0.3 * jnp.ones((16,), jnp.float32), (32, 128))
        _ctx_1024t = jnp.einsum('bsk,bkd->bsd', _ctx_1024c, _ctx_1024P)
        _ctx_1024t = _ctx_1024t * jax.lax.rsqrt(jnp.mean(jnp.square(_ctx_1024t)) + 1e-12) * 0.953939
        ctx_1024 = 4.13588e-05 + 0.999923 * (_ctx_1024t + 0.3 * jax.random.normal(jax.random.fold_in(_rk, 611), (32, 128, 128), jnp.float32))
        _validS = jnp.arange(128)[None, :] < _lenS[:, None]
        _validS2 = jnp.arange(128)[None, :] < _lenS2[:, None]
        _causal = jnp.tril(jnp.ones((128, 128), dtype=bool))
        mask_BxSxS2_ik1 = jnp.where(jnp.broadcast_to(_validS2[:, None, :], (32, 128, 128)), 1, 0).astype(jnp.int32)
        return (x, ctx_1024, mask_BxSxS2_ik1)
    x, ctx_1024, mask_BxSxS2_ik1 = _rec_inputs()

    def _L0_xattn_setup():
        import jax, jax.numpy as jnp
        import numpy as np
        import math
        DIM = 128
        NUM_HEAD = 16
        D_K = DIM // NUM_HEAD
        key = jax.random.key(seed)
        ks = jax.random.split(key, 12)
        B, T = (4, 256)
        s = 1.0 / math.sqrt(DIM)
        inp = {'q': jax.random.normal(ks[0], (B, T, DIM), jnp.float32), 'k': jax.random.normal(ks[1], (B, T, DIM), jnp.float32), 'v': jax.random.normal(ks[2], (B, T, DIM), jnp.float32), 'mask': jax.random.randint(ks[3], (B, T, T), 0, 2, jnp.int32), 'Wq': jax.random.normal(ks[4], (DIM, DIM), jnp.float32) * s, 'bq': jnp.zeros((DIM,), jnp.float32), 'Wk': jax.random.normal(ks[5], (DIM, DIM), jnp.float32) * s, 'bk': jnp.zeros((DIM,), jnp.float32), 'Wv': jax.random.normal(ks[6], (DIM, DIM), jnp.float32) * s, 'bv': jnp.zeros((DIM,), jnp.float32), 'Wo': jax.random.normal(ks[7], (DIM, DIM), jnp.float32) * s, 'bo': jnp.zeros((DIM,), jnp.float32)}
        return inp
    _L0_xattn_all = _L0_xattn_setup()
    _L0_xattn_in = {k: v for k, v in _L0_xattn_all.items() if k in ('Wq', 'bq', 'Wk', 'bk', 'Wv', 'bv', 'Wo', 'bo')}
    del _L0_xattn_all

    def _L0_ffn_setup():
        import jax, jax.numpy as jnp
        import numpy as np
        H = 128
        I = 88
        E = 64
        TOP_K = 8
        NG = 8
        TOPK_GROUP = 4
        N_SHARED = 2
        ROUTED_SCALE = 2.5
        S_I = I * N_SHARED

        def _route(x, gate_w, gate_bias):
            T = x.shape[0]
            logits = x @ gate_w.T
            scores = jax.nn.sigmoid(logits)
            scores_for_choice = scores + gate_bias[None, :]
            grp = scores_for_choice.reshape(T, NG, E // NG)
            group_scores = jnp.sum(jax.lax.top_k(grp, 2)[0], axis=-1)
            _, gidx = jax.lax.top_k(group_scores, TOPK_GROUP)
            gmask = jnp.zeros((T, NG), dtype=scores.dtype).at[jnp.arange(T)[:, None], gidx].set(1.0)
            emask = jnp.repeat(gmask, E // NG, axis=1)
            masked = jnp.where(emask > 0, scores_for_choice, 0.0)
            _, topk_idx = jax.lax.top_k(masked, TOP_K)
            topk_w = jnp.take_along_axis(scores, topk_idx, axis=1)
            topk_w = topk_w / (jnp.sum(topk_w, axis=-1, keepdims=True) + 1e-20)
            topk_w = topk_w * ROUTED_SCALE
            rw = jnp.zeros((T, E), dtype=scores.dtype).at[jnp.arange(T)[:, None], topk_idx].add(topk_w)
            return rw

        def _mlp(x, gw, uw, dw):
            return jax.nn.silu(x @ gw.T) * (x @ uw.T) @ dw.T
        key = jax.random.key(seed)
        ks = jax.random.split(key, 10)
        sc = 0.02
        return {'hidden_states': jax.random.normal(ks[0], (1, 128, H), dtype=jnp.float32), 'gate_w': sc * jax.random.normal(ks[1], (E, H), dtype=jnp.float32), 'gate_bias': sc * jax.random.normal(ks[2], (E,), dtype=jnp.float32), 'Wg': sc * jax.random.normal(ks[3], (E, I, H), dtype=jnp.float32), 'Wu': sc * jax.random.normal(ks[4], (E, I, H), dtype=jnp.float32), 'Wd': sc * jax.random.normal(ks[5], (E, H, I), dtype=jnp.float32), 'Sg': sc * jax.random.normal(ks[6], (S_I, H), dtype=jnp.float32), 'Su': sc * jax.random.normal(ks[7], (S_I, H), dtype=jnp.float32), 'Sd': sc * jax.random.normal(ks[8], (H, S_I), dtype=jnp.float32)}
    _L0_ffn_all = _L0_ffn_setup()
    _L0_ffn_in = {k: v for k, v in _L0_ffn_all.items() if k in ('gate_w', 'gate_bias', 'Wg', 'Wu', 'Wd', 'Sg', 'Su', 'Sd')}
    del _L0_ffn_all
    return {'x': x, 'ctx_1024': ctx_1024, 'mask_BxSxS2_ik1': mask_BxSxS2_ik1, 'L0_xattn_Wq': _L0_xattn_in['Wq'], 'L0_xattn_bq': _L0_xattn_in['bq'], 'L0_xattn_Wk': _L0_xattn_in['Wk'], 'L0_xattn_bk': _L0_xattn_in['bk'], 'L0_xattn_Wv': _L0_xattn_in['Wv'], 'L0_xattn_bv': _L0_xattn_in['bv'], 'L0_xattn_Wo': _L0_xattn_in['Wo'], 'L0_xattn_bo': _L0_xattn_in['bo'], 'L0_ffn_gate_w': _L0_ffn_in['gate_w'], 'L0_ffn_gate_bias': _L0_ffn_in['gate_bias'], 'L0_ffn_Wg': _L0_ffn_in['Wg'], 'L0_ffn_Wu': _L0_ffn_in['Wu'], 'L0_ffn_Wd': _L0_ffn_in['Wd'], 'L0_ffn_Sg': _L0_ffn_in['Sg'], 'L0_ffn_Su': _L0_ffn_in['Su'], 'L0_ffn_Sd': _L0_ffn_in['Sd']}

def reference(x, ctx_1024, mask_BxSxS2_ik1, L0_xattn_Wq, L0_xattn_bq, L0_xattn_Wk, L0_xattn_bk, L0_xattn_Wv, L0_xattn_bv, L0_xattn_Wo, L0_xattn_bo, L0_ffn_gate_w, L0_ffn_gate_bias, L0_ffn_Wg, L0_ffn_Wu, L0_ffn_Wd, L0_ffn_Sg, L0_ffn_Su, L0_ffn_Sd):
    import jax
    import jax.numpy as jnp

    def _L0_xattn_ref(q, k, v, mask, Wq, bq, Wk, bk, Wv, bv, Wo, bo):
        import jax, jax.numpy as jnp
        import numpy as np
        import math
        DIM = 128
        NUM_HEAD = 16
        D_K = DIM // NUM_HEAD
        B, T, _ = q.shape

        def proj(x, W, b):
            y = x @ W.T + b
            return y.reshape(B, -1, NUM_HEAD, D_K).transpose(0, 2, 1, 3)
        qh = proj(q, Wq, bq)
        kh = proj(k, Wk, bk)
        vh = proj(v, Wv, bv)
        score = jnp.einsum('bhtd,bhsd->bhts', qh, kh) / math.sqrt(D_K)
        score = jnp.where(mask[:, None, :, :] == 0, jnp.float32(-60000.0), score)
        attn = jax.nn.softmax(score, axis=-1)
        out = jnp.einsum('bhts,bhsd->bhtd', attn, vh)
        out = out.transpose(0, 2, 1, 3).reshape(B, -1, DIM)
        return out @ Wo.T + bo

    def _L0_ffn_ref(hidden_states, gate_w, gate_bias, Wg, Wu, Wd, Sg, Su, Sd):
        import jax, jax.numpy as jnp
        import numpy as np
        H = 128
        I = 88
        E = 64
        TOP_K = 8
        NG = 8
        TOPK_GROUP = 4
        N_SHARED = 2
        ROUTED_SCALE = 2.5
        S_I = I * N_SHARED

        def _route(x, gate_w, gate_bias):
            T = x.shape[0]
            logits = x @ gate_w.T
            scores = jax.nn.sigmoid(logits)
            scores_for_choice = scores + gate_bias[None, :]
            grp = scores_for_choice.reshape(T, NG, E // NG)
            group_scores = jnp.sum(jax.lax.top_k(grp, 2)[0], axis=-1)
            _, gidx = jax.lax.top_k(group_scores, TOPK_GROUP)
            gmask = jnp.zeros((T, NG), dtype=scores.dtype).at[jnp.arange(T)[:, None], gidx].set(1.0)
            emask = jnp.repeat(gmask, E // NG, axis=1)
            masked = jnp.where(emask > 0, scores_for_choice, 0.0)
            _, topk_idx = jax.lax.top_k(masked, TOP_K)
            topk_w = jnp.take_along_axis(scores, topk_idx, axis=1)
            topk_w = topk_w / (jnp.sum(topk_w, axis=-1, keepdims=True) + 1e-20)
            topk_w = topk_w * ROUTED_SCALE
            rw = jnp.zeros((T, E), dtype=scores.dtype).at[jnp.arange(T)[:, None], topk_idx].add(topk_w)
            return rw

        def _mlp(x, gw, uw, dw):
            return jax.nn.silu(x @ gw.T) * (x @ uw.T) @ dw.T
        B, S, _ = hidden_states.shape
        x = hidden_states.reshape(B * S, H)
        rw = _route(x, gate_w, gate_bias)
        expert_out = jax.vmap(lambda gw_, uw_, dw_: _mlp(x, gw_, uw_, dw_))(Wg, Wu, Wd)
        routed = jnp.einsum('eth,te->th', expert_out, rw)
        shared = _mlp(x, Sg, Su, Sd)
        out = (routed + shared).reshape(B, S, H)
        return out
    x = x + _L0_xattn_ref(_layernorm(x, axis=-1), ctx_1024, ctx_1024, mask_BxSxS2_ik1, L0_xattn_Wq, L0_xattn_bq, L0_xattn_Wk, L0_xattn_bk, L0_xattn_Wv, L0_xattn_bv, L0_xattn_Wo, L0_xattn_bo)
    x = x + _L0_ffn_ref(_layernorm(x, axis=-1), L0_ffn_gate_w, L0_ffn_gate_bias, L0_ffn_Wg, L0_ffn_Wu, L0_ffn_Wd, L0_ffn_Sg, L0_ffn_Su, L0_ffn_Sd)
    return x

_drawn_inputs = setup_inputs


def setup_inputs(seed=0):
    import zlib

    import numpy as np

    out = dict(_drawn_inputs(seed))
    spreads = {'L0_xattn_bq': (0.0, 0.341),
     'L0_xattn_bk': (0.0, 0.8),
     'L0_xattn_bv': (0.0, 0.1),
     'L0_xattn_bo': (0.0, 0.1)}
    factors = {'L0_ffn_gate_w': 8.0,
     'L0_ffn_gate_bias': 8.0,
     'L0_ffn_Wg': 8.0,
     'L0_ffn_Wu': 8.0,
     'L0_ffn_Wd': 8.0,
     'L0_ffn_Sg': 8.0,
     'L0_ffn_Su': 8.0,
     'L0_ffn_Sd': 8.0}
    for name, (base, spread) in spreads.items():
        noise = np.random.default_rng([zlib.crc32(name.encode()), seed]).standard_normal(out[name].shape)
        drawn = base * np.exp(spread * noise) if base else spread * noise
        out[name] = jnp.asarray(drawn.astype(out[name].dtype))
    for name, factor in factors.items():
        out[name] = (out[name] * factor).astype(out[name].dtype)
    return out
```

```python
import numpy as np
import concourse.bass as bass
from concourse import mybir
from contextlib import ExitStack

F32, F16, BF16, I32 = mybir.dt.float32, mybir.dt.float16, mybir.dt.bfloat16, mybir.dt.int32
ALU = mybir.AluOpType
ACT = mybir.ActivationFunctionType
AX = mybir.AxisListType

B, T, D = 32, 128, 128
NH, DK = 16, 8
NE, EI, SI = 64, 88, 176
NG, GE, GK, TK = 8, 8, 4, 8
CB = 4
NC = B // CB
CT = CB * T
HQ = 4
UH = 8
NU = CB * NH // UH
VW = DK + 1
RR = NE * EI // 128
RS = -(-SI // 128)
RB = RR + RS
WC = RB * 128
NP, PC = 12, 3 * WC // 12
EPS = 1e-5
MASKED = -(2.0 ** 64)
PICKED = -3.0e38
ROUTED_SCALE = 2.5
RU = 4

CHAIN_FIRST, CHAIN_INNER = 9, 32


def wait(eng, sem, value):
    if isinstance(value, int) and value <= 0:
        return
    eng.wait_ge(sem, value)


def build(nc, x, ctx_in, mask, wq, wk, wv, wo, bq, bk, bv, bo, gate_w, gate_b,
          w_all, consts, onehot, out):
    ctx = ExitStack()
    with ctx:
        def sb(name, shape, dt):
            return ctx.enter_context(nc.sbuf_tensor(name, shape, dt))

        def sem(name):
            return ctx.enter_context(nc.semaphore(name))

        x_v = x.rearrange("(c b) t d -> c t b d", b=CB)
        c_v = ctx_in.rearrange("(c b) t d -> c t b d", b=CB)
        m_v = mask.rearrange("(c b) t s -> c t b s", b=CB)
        out_v = out.rearrange("(c b) t d -> c t b d", b=CB)

        cst = sb("cst", [128, 128 + 4 + 4 + 64], F32)
        ident, qmask, amask, tri = cst[:, 0:128], cst[:, 128:132], cst[:, 132:136], cst[:, 136:200]
        ident_b = sb("ident_b", [128, 128], BF16)
        ident_h = sb("ident_h", [128, 128], F16)
        ones_b = sb("ones_b", [128, 128], BF16)
        augmask = sb("augmask", [128, HQ, T], BF16)
        wq_s, wk_s = sb("wq_s", [128, 128], F32), sb("wk_s", [128, 128], F32)
        wv_s, wo_s = sb("wv_s", [128, 128], F32), sb("wo_s", [128, 128], F32)
        gw_s = sb("gw_s", [128, NE], F32)
        bq_s, bk_s = sb("bq_s", [128, 1], F32), sb("bk_s", [128, 1], F32)
        bv_s, bo_s = sb("bv_s", [128, 128], F32), sb("bo_s", [128, 128], F32)
        gb_s = sb("gb_s", [128, NE], F32)
        onehot_s = sb("onehot_s", [128, RR * 128], F16)

        w_hi, w_lo = sb("w_hi", [128, 3 * WC], F16), sb("w_lo", [128, 3 * WC], F16)
        x2 = sb("x2", [128, NC * CT], F32)
        x2t_hi = sb("x2t_hi", [128, NC * CT], F16)
        x2t_lo = sb("x2t_lo", [128, NC * CT], F16)
        rwt = sb("rwt", [128, NC * CT], F16)

        x_in, c_in = sb("x_in", [128, CB, D], F32), sb("c_in", [128, CB, D], F32)
        m_in = sb("m_in", [128, CB, T], I32)
        mbias = sb("mbias", [128, CB, T], BF16)
        w_in = sb("w_in", [128, 2, PC], F32)
        stats = sb("stats", [128, CB, 6], F32)
        mv, mv2 = sb("mv", [128, CB, 2], F32), sb("mv2", [128, CB, 2], F32)
        var, var2 = sb("var", [128, CB], F32), sb("var2", [128, CB], F32)
        rstd, rstd2 = sb("rstd", [128, CB], F32), sb("rstd2", [128, CB], F32)
        spare_p, spare_v = sb("spare_p", [128, 8], F32), sb("spare_v", [128, 16], F32)
        minus_half = sb("minus_half", [128, CB], F32)
        xn = sb("xn", [128, CB, D], F32)
        xnt, cnt = sb("xnt", [128, CT], F32), sb("cnt", [128, CT], F32)
        qf, kf = sb("qf", [128, CT], F32), sb("kf", [128, CT], F32)
        q_hi, q_lo = sb("q_hi", [128, CB, T], F16), sb("q_lo", [128, CB, T], F16)
        k_hi, k_lo = sb("k_hi", [128, CB, T], F16), sb("k_lo", [128, CB, T], F16)
        qm_hi, qm_lo = sb("qm_hi", [128, HQ, CB, T], F16), sb("qm_lo", [128, HQ, CB, T], F16)
        km_hi = sb("km_hi", [128, HQ, CB, T], F16)
        v_st = sb("v_st", [128, CB, D], F32)
        v_s = sb("v_s", [128, CB, NH, VW], F32)
        negmax = sb("negmax", [128, 128], BF16)
        aug = sb("aug", [128, HQ, T], BF16)
        p_s = sb("p_s", [128, 2, UH * T], F32)
        rsum = sb("rsum", [128, NH], F32)
        o_n = sb("o_n", [128, NH, DK], F32)
        o_t = sb("o_t", [128, CB, T], F32)
        xn2 = sb("xn2", [128, CB, D], F32)
        x2tf = sb("x2tf", [128, CT], F32)
        esig = sb("esig", [128, CB, NE], F32)
        score, choice = sb("score", [128, CB, NE], F32), sb("choice", [128, CB, NE], F32)
        top_a, top_b = sb("top_a", [128, CB * NG, 4], F32), sb("top_b", [128, CB * NG, 4], F32)
        top_c, top_d = sb("top_c", [128, CB * NG, 4], F32), sb("top_d", [128, CB * NG, 4], F32)
        gscore = sb("gscore", [128, CB, NG], F32)
        cmp_a, cmp_b = sb("cmp_a", [128, CB, NG * NG], F32), sb("cmp_b", [128, CB, NG * NG], F32)
        gkeep = sb("gkeep", [128, CB, NG], F32)
        best = sb("best", [128, CB, TK], F32)
        rest = sb("rest", [128, CB, NE], F32)
        wsum = sb("wsum", [128, CB], F32)
        rw = sb("rw", [128, CB, NE], F32)
        rwcat = sb("rwcat", [128, CB, 2, NE], F16)

        sg, gu = p_s[:, :, 0:CT], p_s[:, :, CT:2 * CT]
        h_f = qm_hi[:, :, :, :].rearrange("p h b t -> p (h b t)").bitcast(F32).rearrange("p (k n) -> p k n", k=2)
        h_parts = km_hi[:, :, :, :].rearrange("p h b t -> p (h b t)").rearrange("p (a k n) -> p a k n", a=2, k=2)
        h_hi, h_lo = h_parts[:, 0], h_parts[:, 1]
        y_s, o_st = xnt, xn

        ps = ctx.enter_context(nc.psum_tensor("ps", [128, 8 * 512], F32))

        def bank(n, k=1):
            return ps[:, 512 * n:512 * (n + k)]

        s_const = sem("const_loaded")
        s_prep = sem("constants_prepared")
        s_x, s_c, s_m, s_w = sem("x_loaded"), sem("ctx_loaded"), sem("mask_loaded"), sem("weights_loaded")
        s_oh = sem("onehot_loaded")
        s_wsplit = sem("weights_split")
        s_xb = sem("residual_base_made")
        s_mb = sem("mask_bias_made")
        s_vc = sem("chain_vector")
        s_ac = sem("chain_scalar")
        s_pc = sem("chain_pool")
        s_var, s_rs = sem("x_variance"), sem("x_deviation")
        s_var2, s_rs2 = sem("x2_variance"), sem("x2_deviation")
        s_xn = sem("x_normalised")
        s_b6 = sem("bank6_read")
        s_xt, s_ct, s_qp, s_kp = sem("x_transposed"), sem("ctx_transposed"), sem("q_projected"), sem("k_projected")
        s_vp = sem("v_projected")
        s_xnt, s_cnt = sem("xnt_copied"), sem("cnt_copied")
        s_qf, s_kf = sem("q_copied"), sem("k_copied")
        s_qh, s_kh = sem("q_high"), sem("k_high")
        s_qk = sem("q_k_parts_ready")
        s_vst, s_v = sem("v_staged"), sem("v_ready")
        s_sc, s_max = sem("scores_ready"), sem("max_taken")
        s_mxt, s_aug = sem("max_transposed"), sem("aug_ready")
        s_sts, s_st = sem("key_scores_summed"), sem("exponents_ready")
        s_exp, s_pv = sem("probs_ready"), sem("pv_done")
        s_on, s_ot, s_otc = sem("heads_normalised"), sem("heads_transposed"), sem("heads_copied")
        s_wo, s_x2 = sem("attention_out"), sem("residual_added")
        s_xn2, s_x2t, s_x2f = sem("x2_normalised"), sem("x2_transposed"), sem("x2t_copied")
        s_x2h, s_x2l = sem("x2t_high"), sem("x2t_low")
        s_gl, s_es = sem("gate_logits"), sem("gate_exp")
        s_rw, s_rwt, s_rwc = sem("routing_ready"), sem("routing_transposed"), sem("routing_copied")
        s_gu = sem("gate_up_ready")
        s_rwe = sem("routing_expanded")
        s_sg, s_gup = sem("silu_ready"), sem("gate_times_up")
        s_h, s_hh, s_hl = sem("hidden_ready"), sem("hidden_high"), sem("hidden_low")
        s_d = sem("down_done")
        s_yc, s_yt, s_fin, s_out = sem("y_copied"), sem("y_transposed"), sem("output_made"), sem("output_stored")

        block = ctx.enter_context(nc.Block())

        USES_FIRST = ["xt", "ct", "ot0", "q", "ot1", "k", "ot2"]
        USES_INNER = ["ot3", "xt", "wo", "ct", "ot0", "x2t", "gate", "q", "ot1", "k", "ot2", "rwt"]
        USES_LAST = ["ot3", "wo", "ot0", "x2t", "gate", "ot1", "ot2", "rwt"]
        USES_TAIL = ["ot3", "wo", "x2t", "gate", "rwt"]

        def kind(c):
            return "first" if isinstance(c, int) and c == 0 else "last" if isinstance(c, int) else "inner"

        def bank6_count(c, use):
            if isinstance(c, str) and c == "tail":
                return 12 * (NC - 1) - 1 + len(USES_LAST) + USES_TAIL.index(use)
            if isinstance(c, str) and c == "head":
                return ["xt", "ct", "q", "k"].index(use)
            uses = {"first": USES_FIRST, "inner": USES_INNER, "last": USES_LAST}[kind(c)]
            before = 4 if kind(c) == "first" else 12 * c - 1
            return before + uses.index(use)

        @block.sync
        def _(sp):
            for dst, src in ((cst[:, :], consts), (wq_s[:, :], wq), (wk_s[:, :], wk), (wv_s[:, :], wv),
                             (wo_s[:, :], wo), (gw_s[:, :], gate_w), (bq_s[:, :], bq), (bk_s[:, :], bk)):
                sp.dma_start(dst, src).then_inc(s_const, 16)
            for dst, src in ((bv_s[:, :], bv), (bo_s[:, :], bo), (gb_s[:, :], gate_b)):
                sp.dma_start(dst, src.partition_broadcast(128)).then_inc(s_const, 16)
            sp.dma_start(x_in[:, :, :], x_v[0]).then_inc(s_x, 16)
            sp.dma_start(c_in[:, :, :], c_v[0]).then_inc(s_c, 16)
            sp.dma_start(m_in[:, :, :], m_v[0]).then_inc(s_m, 16)
            sp.dma_start(onehot_s[:, :], onehot).then_inc(s_oh, 16)

            def weights(c):
                for k in range(2):
                    wait(sp, s_wsplit, 2 * c - 3 + k)
                    sp.dma_start(w_in[:, k, :], w_all[:, bass.ds((2 * c - 2 + k) * PC, PC)]).then_inc(s_w, 16)

            def loads(c):
                wait(sp, s_xn, c + 1)
                wait(sp, s_xb, c + 1)
                sp.dma_start(x_in[:, :, :], x_v[bass.ds(c + 1, 1)].squeeze(0)).then_inc(s_x, 16)
                wait(sp, s_ct, c + 1)
                sp.dma_start(c_in[:, :, :], c_v[bass.ds(c + 1, 1)].squeeze(0)).then_inc(s_c, 16)
                wait(sp, s_mb, 2 * c + 2)
                sp.dma_start(m_in[:, :, :], m_v[bass.ds(c + 1, 1)].squeeze(0)).then_inc(s_m, 16)

            loads(0)
            weights(1)
            with sp.Fori(1, NC - 2) as c:
                loads(c)
                weights(c + 1)
            loads(NC - 2)
            for c in range(NC):
                sp.wait_ge(s_fin, c + 1)
                sp.dma_start(out_v[c], o_st[:, :, :]).then_inc(s_out, 16)
                sp.wait_ge(s_out, 16 * (c + 1))

        @block.gpsimd
        def _(pool):
            g = nc.gpsimd

            spare = {}

            def carry_wait(place):
                k = spare.setdefault(place, len(spare))
                g.tensor_tensor(spare_p[:, k:k + 1], minus_half[:, 0:1], minus_half[:, 1:2], ALU.add)

            g.memset(ones_b[:, :], 1.0).then_inc(s_prep, 1)
            g.memset(negmax[:, :], 0.0).then_inc(s_prep, 1)
            g.memset(v_s[:, :, :, :], 1.0).then_inc(s_prep, 1)
            g.memset(augmask[:, :, :], 1.0).then_inc(s_pc, 1)
            g.memset(minus_half[:, :], -0.5).then_inc(s_pc, 1)
            pool.wait_ge(s_const, 16 * 11)
            g.tensor_copy(ident_b[:, :], ident).then_inc(s_prep, 1)
            g.tensor_copy(ident_h[:, :], ident).then_inc(s_prep, 1)
            pool.wait_ge(s_pc, 2)
            for h in range(HQ):
                g.tensor_scalar(augmask[:, h, :], augmask[:, h, :], amask[:, h:h + 1], None, ALU.mult).then_inc(s_prep, 1)

            def prepare(c, lo, hi):
                carry_wait(("mask", lo))
                g.tensor_scalar(mbias[:, lo:hi, :], m_in[:, lo:hi, :], 0.0, MASKED,
                                ALU.is_equal, ALU.mult).then_inc(s_mb, 1)

            def base(c):
                bo_b = bo_s[:, :].unsqueeze(1).to_broadcast([128, CB, D])
                g.tensor_tensor(x2[:, bass.ds(c * CT, CT)].rearrange("p (b d) -> p b d", b=CB), x_in[:, :, :], bo_b,
                                ALU.add).then_inc(s_xb, 1)

            def v_copy(c):
                wait(pool, s_vst, c + 1)
                wait(pool, s_pv, NU * c)
                carry_wait("v")
                g.tensor_copy(v_s[:, :, :, 0:DK], v_st[:, :, :].rearrange("p b (h e) -> p b h e", h=NH))\
                    .then_inc(s_v, 1)

            def deviation(c):
                pool.wait_ge(s_var, c + 1)
                wait(pool, s_xn, c)
                g.tensor_tensor(rstd[:, :], var[:, :], minus_half[:, :], ALU.pow).then_inc(s_rs, 1)

            def deviation2(c):
                pool.wait_ge(s_var2, c + 1)
                wait(pool, s_xn2, c)
                g.tensor_tensor(rstd2[:, :], var2[:, :], minus_half[:, :], ALU.pow).then_inc(s_rs2, 1)

            pool.wait_ge(s_x, 16)
            deviation(0)
            base(0)
            pool.wait_ge(s_m, 16)
            prepare(0, 0, CB - 1)
            prepare(0, CB - 1, CB)
            pool.wait_ge(s_prep, 3)
            v_copy(0)

            def split(c, k):
                pool.wait_ge(s_w, 16 * (2 * c - 2 + k + 1))
                at = bass.ds((2 * c - 2 + k) * PC, PC)
                carry_wait(("weights", k))
                g.tensor_copy(w_hi[:, at], w_in[:, k, :]).then_inc(s_pc, 1)
                pool.wait_ge(s_pc, 2 * c - 2 + k + 3)
                g.tensor_tensor(w_lo[:, at], w_in[:, k, :], w_hi[:, at], ALU.subtract).then_inc(s_wsplit, 1)

            def chunk(c, inner):
                deviation(c + 1)
                if inner:
                    split(c, 0)
                    deviation2(c - 1)
                    split(c, 1)
                pool.wait_ge(s_x, 16 * (c + 2))
                base(c + 1)
                pool.wait_ge(s_m, 16 * (c + 2))
                pool.wait_ge(s_st, NU * c + 6)
                prepare(c + 1, 0, CB - 1)
                pool.wait_ge(s_st, NU * c + 8)
                prepare(c + 1, CB - 1, CB)
                v_copy(c + 1)

            chunk(0, False)
            with pool.Fori(1, NC - 1) as c:
                chunk(c, True)
            deviation2(NC - 2)
            deviation2(NC - 1)

            def low(n, k):
                pool.wait_ge(s_h, n + 1)
                pool.wait_ge(s_hh, n + 1)
                wait(pool, s_d, n - 1)
                g.tensor_tensor(h_lo[:, k % 2, :], h_f[:, k % 2, :], h_hi[:, k % 2, :], ALU.subtract).then_inc(s_hl, 1)

            def low_chunk(c):
                low(c * RB, 0)
                low(c * RB + 1, 1)
                with pool.Fori(0, RR // RU) as turn:
                    r = turn * RU
                    for k in range(RU):
                        low(c * RB + r + (RS + k), k)

            low_chunk(0)
            with pool.Fori(1, NC) as c:
                low_chunk(c)

        @block.scalar
        def _(act):
            a = nc.scalar

            def copy_xnt(c):
                wait(act, s_xt, c + 1)
                wait(act, s_qp, c)
                a.activation(xnt[:, :], bank(6), ACT.Copy).then_inc(s_b6, 1)

            def copy_cnt(c):
                wait(act, s_ct, c + 1)
                wait(act, s_kp, c)
                wait(act, s_vp, c)
                a.activation(cnt[:, :], bank(6), ACT.Copy).then_inc(s_b6, 1)

            def copy_q(c):
                wait(act, s_qp, c + 1)
                wait(act, s_qk, c)
                a.activation(qf[:, :], bank(6), ACT.Identity, bias=bq_s[:, 0:1]).then_inc(s_b6, 1)

            def copy_k(c):
                wait(act, s_kp, c + 1)
                wait(act, s_qk, c)
                a.activation(kf[:, :], bank(6), ACT.Identity, bias=bk_s[:, 0:1]).then_inc(s_b6, 1)

            def high_q(c, done):
                wait(act, s_b6, done)
                wait(act, s_sc, NU * c)
                a.activation(q_hi[:, :, :].rearrange("p b t -> p (b t)"), qf[:, :], ACT.Copy).then_inc(s_qh, 1)

            def high_k(c, done):
                wait(act, s_b6, done)
                wait(act, s_sts, NU * c)
                a.activation(k_hi[:, :, :].rearrange("p b t -> p (b t)"), kf[:, :], ACT.Copy).then_inc(s_kh, 1)

            def exp(c, u):
                n = NU * c + u
                wait(act, s_st, n + 1)
                wait(act, s_pv, n - 1)
                a.activation(p_s[:, u % 2, :], bank(2 + 2 * (u % 2), 2), ACT.Exp, scale=DK ** -0.5).then_inc(s_exp, 1)

            def copy_ot(c, b):
                wait(act, s_ot, CB * c + b + 1)
                wait(act, s_wo, c)
                a.activation(o_t[:, b, :], bank(6)[:, 0:T], ACT.Copy).then_inc(s_b6, 1)

            def copy_x2t(c, done):
                wait(act, s_x2t, c + 1)
                wait(act, s_gl, c)
                wait(act, s_x2l, c)
                a.activation(x2tf[:, :], bank(6), ACT.Copy).then_inc(s_b6, 1)
                wait(act, s_b6, done)
                a.activation(x2t_hi[:, bass.ds(c * CT, CT)], x2tf[:, :], ACT.Copy).then_inc(s_x2h, 1)

            def exp_gate(c):
                wait(act, s_gl, c + 1)
                wait(act, s_rw, c)
                a.activation(esig[:, :, :].rearrange("p b e -> p (b e)"), bank(6)[:, 0:CB * NE], ACT.Exp,
                             scale=-1.0).then_inc(s_b6, 1)

            def copy_rwt(c):
                wait(act, s_rwt, c + 1)
                src = bank(6)[:, 0:CT // 2].bitcast(F16)
                a.activation(rwt[:, bass.ds(c * CT, CT)], src, ACT.Copy).then_inc(s_b6, 1)

            act.wait_ge(s_const, 16 * 11)
            copy_xnt(0)
            copy_cnt(0)
            copy_q(0)
            copy_k(0)
            high_q(0, 3)
            high_k(0, 4)

            def chunk(c, prev, nxt):
                exp(c, 0)
                if prev:
                    copy_ot(c - 1, 3)
                exp(c, 1)
                if nxt:
                    copy_xnt(c + 1)
                exp(c, 2)
                if nxt:
                    copy_cnt(c + 1)
                copy_ot(c, 0)
                exp(c, 3)
                if prev:
                    copy_x2t(c - 1, bank6_count(c, "x2t") + 1)
                exp(c, 4)
                if prev:
                    exp_gate(c - 1)
                if nxt:
                    copy_q(c + 1)
                copy_ot(c, 1)
                exp(c, 5)
                if nxt:
                    copy_k(c + 1)
                exp(c, 6)
                if nxt:
                    high_q(c + 1, bank6_count(c, "q") + 1)
                copy_ot(c, 2)
                if nxt:
                    high_k(c + 1, bank6_count(c, "k") + 1)
                exp(c, 7)
                if prev:
                    copy_rwt(c - 1)

            chunk(0, False, True)
            with act.Fori(1, NC - 1) as c:
                chunk(c, True, True)
            chunk(NC - 1, True, False)
            copy_ot(NC - 1, 3)
            copy_x2t(NC - 1, bank6_count("tail", "x2t") + 1)
            exp_gate(NC - 1)
            copy_rwt(NC - 1)

            def silu(n, k):
                act.wait_ge(s_gu, n + 1)
                wait(act, s_gup, n - 1)
                a.activation(sg[:, k % 2, :], bank(k % 2), ACT.Silu).then_inc(s_sg, 1)

            def high(n, k):
                act.wait_ge(s_h, n + 1)
                wait(act, s_d, n - 1)
                a.activation(h_hi[:, k % 2, :], h_f[:, k % 2, :], ACT.Copy).then_inc(s_hh, 1)

            def y_copy(c):
                wait(act, s_d, RB * (c + 1))
                wait(act, s_yt, c)
                a.activation(y_s[:, :], bank(6), ACT.Copy).then_inc(s_yc, 1)

            def ffn_chunk(c, prev):
                silu(c * RB, 0)
                if prev:
                    high(c * RB - 1, 1)
                silu(c * RB + 1, 1)
                high(c * RB, 0)
                if prev:
                    y_copy(c - 1)
                with act.Fori(0, RR // RU) as turn:
                    r = turn * RU
                    for k in range(RU):
                        n = c * RB + r + (RS + k)
                        silu(n, k)
                        high(n - 1, k + 1)

            ffn_chunk(0, False)
            with act.Fori(1, NC) as c:
                ffn_chunk(c, True)
            high(NC * RB - 1, 1)
            y_copy(NC - 1)

        @block.vector
        def _(dve):
            v = nc.vector

            spare = {}

            def carry_wait(place):
                k = spare.setdefault(place, len(spare))
                v.memset(spare_v[:, k:k + 1], 0.0)

            state = {"base": 0, "k": 0}

            def link(ins):
                ins.then_inc(s_vc, 1)
                state["k"] += 1
                dve.wait_ge(s_vc, state["base"] + state["k"])

            def moments(src, mv_, var_, signal):
                carry_wait(("stats", mv_ is mv))
                for b in range(CB):
                    ins = v.bn_stats(stats[:, b, :], src(b))
                link(ins)
                carry_wait(("aggregate", mv_ is mv))
                for b in range(CB):
                    ins = v.bn_aggr(mv_[:, b, :], stats[:, b, :])
                link(ins)
                v.tensor_scalar(var_[:, :], mv_[:, :, 1], EPS, None, ALU.add).then_inc(signal, 1)

            def normalise(dst, src, mv_, rstd_, signal):
                for b in range(CB):
                    ins = v.tensor_scalar(dst[:, b, :], src(b), mv_[:, b, 0:1], rstd_[:, b:b + 1],
                                          ALU.subtract, ALU.mult)
                ins.then_inc(signal, 1)

            def x_moments(c):
                wait(dve, s_x, 16 * (c + 1))
                wait(dve, s_rs, c)
                moments(lambda b: x_in[:, b, :], mv, var, s_var)

            def norm_x(c):
                wait(dve, s_rs, c + 1)
                wait(dve, s_xt, c)
                normalise(xn, lambda b: x_in[:, b, :], mv, rstd, s_xn)

            def q_low(c):
                wait(dve, s_qh, c + 1)
                link(v.tensor_tensor(q_lo[:, :, :].rearrange("p b t -> p (b t)"), qf[:, :],
                                     q_hi[:, :, :].rearrange("p b t -> p (b t)"), ALU.subtract))

            def qk_masks(c):
                wait(dve, s_kh, c + 1)
                wait(dve, s_sc, NU * c)
                for h in range(HQ):
                    v.tensor_scalar(km_hi[:, h, :, :], k_hi[:, :, :], qmask[:, h:h + 1], None, ALU.mult)
                wait(dve, s_sts, NU * c)
                v.tensor_tensor(k_lo[:, :, :].rearrange("p b t -> p (b t)"), kf[:, :],
                                k_hi[:, :, :].rearrange("p b t -> p (b t)"), ALU.subtract)
                for h in range(HQ):
                    v.tensor_scalar(qm_hi[:, h, :, :], q_hi[:, :, :], qmask[:, h:h + 1], None, ALU.mult)
                for h in range(HQ):
                    ins = v.tensor_scalar(qm_lo[:, h, :, :], q_lo[:, :, :], qmask[:, h:h + 1], None, ALU.mult)
                ins.then_inc(s_qk, 1)

            def v_stage(c):
                wait(dve, s_vp, c + 1)
                wait(dve, s_v, c)
                v.tensor_tensor(v_st[:, :, :], bank(0).rearrange("p (b d) -> p b d", b=CB),
                                bv_s[:, :].unsqueeze(1).to_broadcast([128, CB, D]), ALU.add).then_inc(s_vst, 1)

            def row_max(c, u):
                n = NU * c + u
                half = u % 2
                wait(dve, s_sc, n + 1)
                wait(dve, s_mxt, n - 1)
                dst = negmax[:, 64 * half:64 * half + 64].rearrange("p (j q) -> p j q", j=2)[:, :, 0:HQ]
                v.tensor_reduce(dst, bank(0, 2).rearrange("p (j h s) -> p j h s", j=2, h=HQ), AX.X, ALU.max,
                                negate=True).then_inc(s_max, 1)

            def aug_rows(c, u):
                n = NU * c + u
                p0 = 64 * (u % 2)
                wait(dve, s_mxt, n + 1)
                wait(dve, s_st, n - 1)
                v.tensor_tensor(aug[p0:p0 + 64, :, :],
                                bank(7)[p0:p0 + 64, 0:T].unsqueeze(1).to_broadcast([64, HQ, T]),
                                augmask[p0:p0 + 64, :, :], ALU.mult).then_inc(s_aug, 1)

            def norm_heads(c, b):
                wait(dve, s_pv, NU * c + 2 * b + 2)
                wait(dve, s_ot, CB * c + b)
                o = bank(7)[:, 256:256 + NH * VW].rearrange("p (h e) -> p h e", e=VW)
                link(v.reciprocal(rsum[:, :], o[:, :, DK]))
                v.tensor_tensor(o_n[:, :, :], o[:, :, 0:DK], rsum[:, :].unsqueeze(2).to_broadcast([128, NH, DK]),
                                ALU.mult).then_inc(s_on, 1)

            def x2_chunk(c):
                return x2[:, bass.ds(c * CT, CT)]

            def residual(c):
                wait(dve, s_wo, c + 1)
                v.tensor_tensor(x2_chunk(c), x2_chunk(c), bank(6), ALU.add).then_inc(s_b6, 1)

            def x2_moments(c, done):
                dve.wait_ge(s_b6, done)
                wait(dve, s_rs2, c)
                moments(lambda b: x2[:, bass.ds(c * CT + b * D, D)], mv2, var2, s_var2)

            def norm_x2(c):
                wait(dve, s_rs2, c + 1)
                wait(dve, s_x2t, c)
                normalise(xn2, lambda b: x2[:, bass.ds(c * CT + b * D, D)], mv2, rstd2, s_xn2)

            def x2t_low(c):
                wait(dve, s_x2h, c + 1)
                v.tensor_tensor(x2t_lo[:, bass.ds(c * CT, CT)], x2tf[:, :], x2t_hi[:, bass.ds(c * CT, CT)],
                                ALU.subtract).then_inc(s_x2l, 1)

            flat = "p b e -> p (b e)"
            quad = "p b (i j) -> p b i j"

            def group_scores(c, done):
                dve.wait_ge(s_b6, done)
                wait(dve, s_rwt, c)
                link(v.tensor_scalar(esig[:, :, :], esig[:, :, :], 1.0, None, ALU.add))
                link(v.reciprocal(score[:, :, :].rearrange(flat), esig[:, :, :].rearrange(flat)))
                link(v.tensor_tensor(choice[:, :, :], score[:, :, :],
                                     gb_s[:, :].unsqueeze(1).to_broadcast([128, CB, NE]), ALU.add))
                m = choice[:, :, :].rearrange(flat).rearrange("p (g e) -> p g e", e=GE)
                v.tensor_tensor(top_a[:, :, :], m[:, :, 0:4], m[:, :, 4:8], ALU.max)
                link(v.tensor_tensor(top_b[:, :, :], m[:, :, 0:4], m[:, :, 4:8], ALU.min))
                a_, b_, c_, d_ = top_a, top_b, top_c, top_d
                for w in (2, 1):
                    v.tensor_tensor(c_[:, :, 0:w], a_[:, :, 0:w], a_[:, :, w:2 * w], ALU.max)
                    v.tensor_tensor(d_[:, :, 0:w], a_[:, :, 0:w], a_[:, :, w:2 * w], ALU.min)
                    link(v.tensor_tensor(d_[:, :, 2:2 + w], b_[:, :, 0:w], b_[:, :, w:2 * w], ALU.max))
                    link(v.tensor_tensor(d_[:, :, 0:w], d_[:, :, 0:w], d_[:, :, 2:2 + w], ALU.max))
                    a_, b_, c_, d_ = c_, d_, a_, b_
                link(v.tensor_tensor(gscore[:, :, :].rearrange("p b g -> p (b g)"), a_[:, :, 0], b_[:, :, 0], ALU.add))

            def keep_groups():
                other = gscore[:, :, :].unsqueeze(2).to_broadcast([128, CB, NG, NG])
                own = gscore[:, :, :].unsqueeze(3).to_broadcast([128, CB, NG, NG])
                v.tensor_tensor(cmp_a[:, :, :].rearrange(quad, i=NG), other, own, ALU.is_gt)
                link(v.tensor_tensor(cmp_b[:, :, :].rearrange(quad, i=NG), other, own, ALU.is_ge))
                link(v.tensor_tensor(cmp_b[:, :, :], cmp_b[:, :, :], tri.unsqueeze(1).to_broadcast([128, CB, NG * NG]),
                                     ALU.mult))
                link(v.tensor_tensor(cmp_a[:, :, :], cmp_a[:, :, :], cmp_b[:, :, :], ALU.max))
                link(v.tensor_reduce(gkeep[:, :, :], cmp_a[:, :, :].rearrange(quad, i=NG), AX.X, ALU.add))
                link(v.tensor_scalar(gkeep[:, :, :], gkeep[:, :, :], float(GK), None, ALU.is_lt))
                link(v.tensor_tensor(choice[:, :, :].rearrange("p b (g e) -> p b g e", e=GE),
                                     choice[:, :, :].rearrange("p b (g e) -> p b g e", e=GE),
                                     gkeep[:, :, :].unsqueeze(3).to_broadcast([128, CB, NG, GE]), ALU.mult))

            def weigh_experts():
                carry_wait("best")
                for b in range(CB):
                    ins = v.max(best[:, b, :], choice[:, b, :])
                link(ins)
                carry_wait("rest")
                for b in range(CB):
                    ins = v.match_replace(rest[:, b, :], best[:, b, :], choice[:, b, :], PICKED)
                link(ins)
                link(v.scalar_tensor_tensor(rw[:, :, :].rearrange(flat), rest[:, :, :].rearrange(flat), PICKED,
                                            score[:, :, :].rearrange(flat), ALU.is_equal, ALU.mult))
                link(v.tensor_reduce(wsum[:, :], rw[:, :, :], AX.X, ALU.add))
                link(v.tensor_scalar(wsum[:, :], wsum[:, :], 1e-20, None, ALU.add))
                link(v.reciprocal(wsum[:, :], wsum[:, :]))
                link(v.scalar_tensor_tensor(rw[:, :, :], rw[:, :, :], ROUTED_SCALE,
                                            wsum[:, :].unsqueeze(2).to_broadcast([128, CB, NE]), ALU.mult, ALU.mult))
                link(v.tensor_copy(rwcat[:, :, 0, :], rw[:, :, :]))
                v.tensor_tensor(rwcat[:, :, 1, :], rw[:, :, :], rwcat[:, :, 0, :], ALU.subtract).then_inc(s_rw, 1)

            dve.wait_ge(s_const, 16 * 11)
            dve.wait_ge(s_prep, 9)
            x_moments(0)
            norm_x(0)
            q_low(0)
            v_stage(0)
            qk_masks(0)

            def chunk(c, prev, nxt):
                row_max(c, 0)
                for u in range(NU):
                    if u == 1 and nxt:
                        norm_x(c + 1)
                    if u == 3 and prev:
                        norm_x2(c - 1)
                    aug_rows(c, u)
                    if u + 1 < NU:
                        row_max(c, u + 1)
                    if u % 2 == 0:
                        if u:
                            norm_heads(c, u // 2 - 1)
                        elif prev:
                            norm_heads(c - 1, CB - 1)
                    if u == 0 and nxt:
                        x_moments(c + 1)
                    if u == 2 and prev:
                        residual(c - 1)
                        x2_moments(c - 1, bank6_count(c, "wo") + 1)
                    if u == 3 and prev:
                        x2t_low(c - 1)
                    if u == 4 and prev:
                        group_scores(c - 1, bank6_count(c, "gate") + 1)
                    if u == 5 and prev:
                        keep_groups()
                    if u == 6 and prev:
                        weigh_experts()
                    if u == 6 and nxt:
                        q_low(c + 1)
                    if u == 7 and nxt:
                        v_stage(c + 1)
                        qk_masks(c + 1)

            chunk(0, False, True)
            assert state["k"] == CHAIN_FIRST, state["k"]
            state["k"] = 0
            with dve.Fori(1, NC - 1) as c:
                state["base"] = CHAIN_FIRST + (c - 1) * CHAIN_INNER
                chunk(c, True, True)
            assert state["k"] == CHAIN_INNER, state["k"]
            state.update(base=CHAIN_FIRST + (NC - 2) * CHAIN_INNER, k=0)
            chunk(NC - 1, True, False)
            norm_heads(NC - 1, CB - 1)
            residual(NC - 1)
            x2_moments(NC - 1, bank6_count("tail", "wo") + 1)
            norm_x2(NC - 1)
            x2t_low(NC - 1)
            group_scores(NC - 1, bank6_count("tail", "gate") + 1)
            keep_groups()
            weigh_experts()

            def gate_up(n, k):
                dve.wait_ge(s_sg, n + 1)
                v.tensor_tensor(gu[:, k % 2, :], sg[:, k % 2, :], bank(2 + k % 2), ALU.mult).then_inc(s_gup, 1)

            def hidden(n, k, routed):
                wait(dve, s_gup, n + 1)
                wait(dve, s_hl, n - 1)
                if routed is None:
                    v.tensor_copy(h_f[:, k % 2, :], gu[:, k % 2, :]).then_inc(s_h, 1)
                else:
                    dve.wait_ge(s_rwe, routed + 1)
                    v.tensor_tensor(h_f[:, k % 2, :], gu[:, k % 2, :], bank(4 + k % 2), ALU.mult).then_inc(s_h, 1)

            def output(c):
                wait(dve, s_yt, c + 1)
                wait(dve, s_out, 16 * c)
                v.tensor_tensor(o_st[:, :, :].rearrange("p b d -> p (b d)"), x2_chunk(c), bank(7),
                                ALU.add).then_inc(s_fin, 1)

            def ffn_chunk(c, prev):
                for k in range(RS):
                    gate_up(c * RB + k, k)
                    hidden(c * RB + k, k, None)
                with dve.Fori(0, RR // RU) as turn:
                    r = turn * RU
                    for k in range(RU):
                        gate_up(c * RB + r + (RS + k), k)
                        hidden(c * RB + r + (RS + k), k, c * RR + r + k)
                if prev:
                    output(c - 1)

            ffn_chunk(0, False)
            with dve.Fori(1, NC) as c:
                ffn_chunk(c, True)
            output(NC - 1)

        @block.tensor
        def _(pe):
            t = nc.tensor

            def heads4(ap):
                return ap.rearrange("p (h t) -> p h t", h=HQ)

            def transpose4(src, done, signal):
                pe.wait_ge(s_b6, done) if not isinstance(done, int) or done > 0 else None
                for b in range(CB):
                    ins = t.transpose(bank(6)[:, b * 128:(b + 1) * 128], src(b), ident)
                ins.then_inc(signal, 1)

            def x_transpose(c, done):
                wait(pe, s_xn, c + 1)
                transpose4(lambda b: xn[:, b, :], done, s_xt)

            def ctx_transpose(c, done):
                wait(pe, s_c, 16 * (c + 1))
                transpose4(lambda b: c_in[:, b, :], done, s_ct)

            def project(w, src, done, signal):
                wait(pe, s_b6, done)
                t.matmul(bank(6), w[:, :], src[:, :], start=True, stop=True).then_inc(signal, 1)

            def project_v(c, done):
                wait(pe, s_b6, done)
                wait(pe, s_max, NU * c)
                for b in range(CB):
                    ins = t.matmul(bank(0)[:, b * 128:(b + 1) * 128], cnt[:, b * 128:(b + 1) * 128], wv_s[:, :],
                                   start=True, stop=True)
                ins.then_inc(s_vp, 1)

            def quadrants(u):
                return [(jj, slice(32 * (2 * (u % 2) + jj), 32 * (2 * (u % 2) + jj) + 32)) for jj in range(2)]

            def scores(c, u):
                n, b = NU * c + u, u // 2
                wait(pe, s_max, n)
                if u == 0:
                    wait(pe, s_qk, c + 1)
                    wait(pe, s_vst, c + 1)
                for jj, q in quadrants(u):
                    t.matmul(heads4(bank(jj)), q_hi[q, b, :], km_hi[q, :, b, :], start=True, stop=False)
                wait(pe, s_mb, 2 * c + (1 if b < CB - 1 else 2))
                for jj, q in quadrants(u):
                    ins = t.matmul(heads4(bank(jj)), ident_b[:, :],
                                   mbias[:, b, :].unsqueeze(1).to_broadcast([128, HQ, T]), start=False, stop=True)
                ins.then_inc(s_sc, 1)

            def key_scores(c, u):
                n, b, first = NU * c + u, u // 2, 2 + 2 * (u % 2)
                wait(pe, s_exp, n - 1)
                for x_, y_ in ((k_hi, qm_hi), (k_hi, qm_lo), (k_lo, qm_hi)):
                    for jj, q in quadrants(u):
                        ins = t.matmul(heads4(bank(first + jj)), x_[q, b, :], y_[q, :, b, :],
                                       start=x_ is k_hi and y_ is qm_hi, stop=False)
                ins.then_inc(s_sts, 1)

            def max_transpose(c, u):
                p0 = 64 * (u % 2)
                wait(pe, s_max, NU * c + u + 1)
                if u % 2:
                    wait(pe, s_on, CB * c + (u - 1) // 2)
                t.matmul(bank(7)[p0:p0 + 64, 0:T], negmax[:, p0:p0 + 64], ident_b[:, :],
                         start=True, stop=True).then_inc(s_mxt, 1)

            def mask_and_max(c, u):
                n, b, first = NU * c + u, u // 2, 2 + 2 * (u % 2)
                for jj, q in quadrants(u):
                    t.matmul(heads4(bank(first + jj)), mbias[:, b, :],
                             ident_b[:, :].unsqueeze(1).to_broadcast([128, HQ, T]), start=False, stop=False)
                wait(pe, s_aug, n + 1)
                for jj, q in quadrants(u):
                    ins = t.matmul(heads4(bank(first + jj)), ones_b[q, :], aug[q, :, :], start=False, stop=True)
                ins.then_inc(s_st, 1)

            def attend(c, u):
                n, b = NU * c + u, u // 2
                wait(pe, s_exp, n + 1)
                if u == 0:
                    wait(pe, s_v, c + 1)
                for hh in range(UH):
                    h = UH * (u % 2) + hh
                    ins = t.matmul(bank(7)[:, 256 + h * VW:256 + (h + 1) * VW], p_s[:, u % 2, hh * T:(hh + 1) * T],
                                   v_s[:, b, h, :], start=True, stop=True)
                ins.then_inc(s_pv, 1)

            def out_transpose(c, b, done):
                wait(pe, s_on, CB * c + b + 1)
                wait(pe, s_b6, done)
                t.transpose(bank(6)[:, 0:128], o_n[:, :, :].rearrange("p h e -> p (h e)"), ident).then_inc(s_ot, 1)

            def attention_out(done):
                wait(pe, s_b6, done)
                for b in range(CB):
                    ins = t.matmul(bank(6)[:, b * 128:(b + 1) * 128], o_t[:, b, :], wo_s[:, :], start=True, stop=True)
                ins.then_inc(s_wo, 1)

            def x2_transpose(c, done):
                wait(pe, s_xn2, c + 1)
                transpose4(lambda b: xn2[:, b, :], done, s_x2t)

            def gate(done):
                wait(pe, s_b6, done)
                for b in range(CB):
                    ins = t.matmul(bank(6)[:, b * NE:(b + 1) * NE], x2tf[:, b * 128:(b + 1) * 128], gw_s[:, :],
                                   start=True, stop=True)
                ins.then_inc(s_gl, 1)

            def routing_transpose(c, done):
                wait(pe, s_rw, c + 1)
                wait(pe, s_b6, done)
                for b in range(CB):
                    ins = t.transpose(bank(6)[:, 64 * b:64 * b + 64].bitcast(F16),
                                      rwcat[:, b, :, :].rearrange("p k e -> p (k e)"), ident_h[:, :])
                ins.then_inc(s_rwt, 1)

            pe.wait_ge(s_const, 16 * 11)
            pe.wait_ge(s_prep, 9)
            x_transpose(0, 0)
            ctx_transpose(0, 1)
            project(wq_s, xnt, 2, s_qp)
            project(wk_s, cnt, 3, s_kp)
            project_v(0, 2)

            def chunk(c, prev, nxt):
                def at(use):
                    return bank6_count(c, use)

                scores(c, 0)
                for u in range(NU):
                    key_scores(c, u)
                    max_transpose(c, u)
                    if u == 1 and prev:
                        out_transpose(c - 1, CB - 1, at("ot3"))
                    if u in (3, 5, 7):
                        out_transpose(c, (u - 3) // 2, at(f"ot{(u - 3) // 2}"))
                    if u + 1 < NU:
                        scores(c, u + 1)
                    mask_and_max(c, u)
                    if u:
                        attend(c, u - 1)
                    elif prev:
                        attend(c - 1, NU - 1)
                    if u == 1 and nxt:
                        x_transpose(c + 1, at("xt"))
                    if u == 2 and prev:
                        attention_out(at("wo"))
                    if u == 2 and nxt:
                        ctx_transpose(c + 1, at("ct"))
                    if u == 3 and prev:
                        x2_transpose(c - 1, at("x2t"))
                    if u == 4 and prev:
                        gate(at("gate"))
                    if u == 4 and nxt:
                        project(wq_s, xnt, at("q"), s_qp)
                    if u == 5 and nxt:
                        project(wk_s, cnt, at("k"), s_kp)
                    if u == 7 and nxt:
                        project_v(c + 1, at("k"))
                    if u == 7 and prev:
                        routing_transpose(c - 1, at("rwt"))

            chunk(0, False, True)
            with pe.Fori(1, NC - 1) as c:
                chunk(c, True, True)
            chunk(NC - 1, True, False)
            attend(NC - 1, NU - 1)
            out_transpose(NC - 1, CB - 1, bank6_count("tail", "ot3"))
            attention_out(bank6_count("tail", "wo"))
            x2_transpose(NC - 1, bank6_count("tail", "x2t"))
            gate(bank6_count("tail", "gate"))
            routing_transpose(NC - 1, bank6_count("tail", "rwt"))

            pe.wait_ge(s_exp, NC * NU)
            pe.wait_ge(s_b6, bank6_count("tail", "rwt") + 1)
            pe.wait_ge(s_x2l, NC)
            pe.wait_ge(s_wsplit, NP)
            pe.wait_ge(s_oh, 16)

            def split_product(out, w_at, a, b, start, stop):
                t.matmul(out, w_hi[:, w_at], a, start=start, stop=False)
                t.matmul(out, w_hi[:, w_at], b, start=False, stop=False)
                return t.matmul(out, w_lo[:, w_at], a, start=False, stop=stop)

            def gate_and_up(n, c, k, block):
                wait(pe, s_sg, n - 1)
                wait(pe, s_gup, n - 1)
                tok = bass.ds(c * CT, CT)
                a, b = x2t_hi[:, tok], x2t_lo[:, tok]
                split_product(bank(k % 2), bass.ds(block * 128, 128), a, b, True, True)
                split_product(bank(2 + k % 2), bass.ds(WC + block * 128, 128), a, b, True, True).then_inc(s_gu, 1)

            def expand(n, c, k, block):
                wait(pe, s_h, n - 1)
                t.matmul(bank(4 + k % 2), onehot_s[:, bass.ds(block * 128, 128)], rwt[:, bass.ds(c * CT, CT)],
                         start=True, stop=True).then_inc(s_rwe, 1)

            def down(n, k, block, start=False, stop=False):
                wait(pe, s_hl, n + 1)
                split_product(bank(6), bass.ds(2 * WC + block * 128, 128), h_hi[:, k % 2, :], h_lo[:, k % 2, :],
                              start, stop).then_inc(s_d, 1)

            def y_transpose(c):
                wait(pe, s_yc, c + 1)
                wait(pe, s_fin, c)
                for b in range(CB):
                    ins = t.transpose(bank(7)[:, b * 128:(b + 1) * 128], y_s[:, b * 128:(b + 1) * 128], ident)
                ins.then_inc(s_yt, 1)

            def ffn_chunk(c, prev):
                n = c * RB
                for k in range(RS):
                    gate_and_up(n + k, c, k, RR + k)
                    if prev:
                        down(n + k - 2, k, RR - 2 + k, stop=k == 1)
                for k in range(RU):
                    gate_and_up(n + RS + k, c, k, k)
                    expand(n + RS + k, c, k, k)
                    if k == 0:
                        wait(pe, s_yc, c)
                    down(n + k, k, RR + k if k < RS else k - RS, start=k == 0)
                with pe.Fori(1, RR // RU) as turn:
                    r = turn * RU
                    for k in range(RU):
                        gate_and_up(n + r + (RS + k), c, k, r + k)
                        expand(n + r + (RS + k), c, k, r + k)
                        down(n + r + k, k, r + (k - RS))
                if prev:
                    y_transpose(c - 1)

            ffn_chunk(0, False)
            with pe.Fori(1, NC) as c:
                ffn_chunk(c, True)
            for k in range(2):
                down(NC * RB - 2 + k, k, RR - 2 + k, stop=k == 1)
            y_transpose(NC - 1)


def kernel(x, ctx_1024, mask_BxSxS2_ik1, L0_xattn_Wq, L0_xattn_bq, L0_xattn_Wk, L0_xattn_bk, L0_xattn_Wv,
           L0_xattn_bv, L0_xattn_Wo, L0_xattn_bo, L0_ffn_gate_w, L0_ffn_gate_bias, L0_ffn_Wg, L0_ffn_Wu,
           L0_ffn_Wd, L0_ffn_Sg, L0_ffn_Su, L0_ffn_Sd):
    import concourse.bacc as bacc
    from concourse.bass_utils import run_bass_kernel_spmd

    a = np.ascontiguousarray
    pad = np.zeros((WC - NE * EI - SI, D), np.float32)
    rows_g = np.concatenate([np.asarray(L0_ffn_Wg).reshape(NE * EI, D), np.asarray(L0_ffn_Sg), pad])
    rows_u = np.concatenate([np.asarray(L0_ffn_Wu).reshape(NE * EI, D), np.asarray(L0_ffn_Su), pad])
    rows_d = np.concatenate([np.asarray(L0_ffn_Wd).transpose(0, 2, 1).reshape(NE * EI, D), np.asarray(L0_ffn_Sd).T, pad])
    w_all = np.concatenate([rows_g.T, rows_u.T, rows_d.reshape(RB, 128, D).transpose(1, 0, 2).reshape(128, RB * D)], 1)

    p = np.arange(128)[:, None]
    g = np.arange(HQ)[None, :]
    i, j = np.divmod(np.arange(NG * NG)[None, :], NG)
    consts = np.concatenate([np.eye(128), (p % 32) // DK == g, p % 32 == g, np.broadcast_to(j < i, (128, NG * NG))],
                            1).astype(np.float32)
    onehot = (p % NE == np.arange(RR * 128)[None, :] // EI).astype(np.float16)

    arrays = {
        "x": np.asarray(x), "ctx": np.asarray(ctx_1024), "mask": np.asarray(mask_BxSxS2_ik1),
        "wq": np.asarray(L0_xattn_Wq).T, "wk": np.asarray(L0_xattn_Wk).T,
        "wv": np.asarray(L0_xattn_Wv).T, "wo": np.asarray(L0_xattn_Wo).T,
        "bq": np.asarray(L0_xattn_bq).reshape(D, 1), "bk": np.asarray(L0_xattn_bk).reshape(D, 1),
        "bv": np.asarray(L0_xattn_bv), "bo": np.asarray(L0_xattn_bo),
        "gate_w": np.asarray(L0_ffn_gate_w).T, "gate_b": np.asarray(L0_ffn_gate_bias),
        "w_all": w_all, "consts": consts, "onehot": onehot,
    }
    arrays = {k + "_dram": a(v) for k, v in arrays.items()}
    nc = bacc.Bacc("TRN2", target_bir_lowering=False, num_devices=1)
    args = [nc.dram_tensor(k, v.shape, mybir.dt.from_np(v.dtype), kind="ExternalInput").ap() for k, v in arrays.items()]
    args.append(nc.dram_tensor("out_dram", (B, T, D), F32, kind="ExternalOutput").ap())
    build(nc, *args)
    r = run_bass_kernel_spmd(nc, [arrays], core_ids=[0])
    return r.results[0]["out_dram"]
```

```python
import numpy as np
import concourse.bass as bass
from concourse import mybir
from contextlib import ExitStack

F32, F16, BF16, I32 = mybir.dt.float32, mybir.dt.float16, mybir.dt.bfloat16, mybir.dt.int32
ALU = mybir.AluOpType
ACT = mybir.ActivationFunctionType
AX = mybir.AxisListType

B, T, D = 32, 128, 128
NH, DK = 16, 8
NE, EI, SI = 64, 88, 176
NG, GE, GK, TK = 8, 8, 4, 8
CB = 4
NC = B // CB
CT = CB * T
HQ = 4
UH = 8
NU = CB * NH // UH
VW = DK + 1
RR = NE * EI // 128
RS = -(-SI // 128)
RB = RR + RS
WC = RB * 128
NP = (NC - 2) * NU
PC = 3 * WC // NP
WB = 4
EPS = 1e-5
MASKED = -(2.0 ** 64)
PICKED = -3.0e38
ROUTED_SCALE = 2.5
RU = 4

CHAIN_FIRST, CHAIN_INNER = 7, 31


def wait(eng, sem, value):
    if isinstance(value, int) and value <= 0:
        return
    eng.wait_ge(sem, value)


def build(nc, x, ctx_in, mask, wq, wk, wv, wo, bq, bk, bv, bo, gate_w, gate_b,
          w_all, consts, sel, onehot, out):
    ctx = ExitStack()
    with ctx:
        def sb(name, shape, dt):
            return ctx.enter_context(nc.sbuf_tensor(name, shape, dt))

        def sem(name):
            return ctx.enter_context(nc.semaphore(name))

        x_v = x.rearrange("(c b) t d -> c t b d", b=CB)
        c_v = ctx_in.rearrange("(c b) t d -> c t b d", b=CB)
        m_v = mask.rearrange("(c b) t s -> c t b s", b=CB)
        out_v = out.rearrange("(c b) t d -> c t b d", b=CB)

        cst = sb("cst", [128, 128 + 4 + 4 + 64], F32)
        ident, qmask, amask, tri = cst[:, 0:128], cst[:, 128:132], cst[:, 132:136], cst[:, 136:200]
        ident_b = sb("ident_b", [128, 128], BF16)
        ident_h = sb("ident_h", [128, 128], F16)
        ones_b = sb("ones_b", [128, 128], BF16)
        augmask = sb("augmask", [128, HQ, T], BF16)
        wq_s, wk_s = sb("wq_s", [128, 128], F32), sb("wk_s", [128, 128], F32)
        wv_s, wo_s = sb("wv_s", [128, 128], F32), sb("wo_s", [128, 128], F32)
        gw_s = sb("gw_s", [128, NE], F32)
        bq_s, bk_s = sb("bq_s", [128, 1], F32), sb("bk_s", [128, 1], F32)
        bv_s, bo_s = sb("bv_s", [128, 128], F32), sb("bo_s", [128, 128], F32)
        gb_s = sb("gb_s", [128, NE], F32)
        onehot_s = sb("onehot_s", [128, RR * 128], F16)
        sel_s = sb("sel_s", [128, 4, 4, 128], F16)
        q_sel, k_sel = (sel_s[:, 0], sel_s[:, 1]), (sel_s[:, 2], sel_s[:, 3])

        w_hi, w_lo = sb("w_hi", [128, 3 * WC], F16), sb("w_lo", [128, 3 * WC], F16)
        x2 = sb("x2", [128, NC * CT], F32)
        x2t_hi = sb("x2t_hi", [128, NC * CT], F16)
        x2t_lo = sb("x2t_lo", [128, NC * CT], F16)
        rwt = sb("rwt", [128, NC * CT], F16)

        x_in, c_in = sb("x_in", [128, CB, D], F32), sb("c_in", [128, CB, D], F32)
        m_in = sb("m_in", [128, CB, T], I32)
        mbias = sb("mbias", [128, CB, T], BF16)
        w_in = sb("w_in", [128, WB, PC], F32)
        stats = sb("stats", [128, CB, 6], F32)
        mv, mv2 = sb("mv", [128, CB, 2], F32), sb("mv2", [128, CB, 2], F32)
        var, var2 = sb("var", [128, CB], F32), sb("var2", [128, CB], F32)
        rstd, rstd2 = sb("rstd", [128, CB], F32), sb("rstd2", [128, CB], F32)
        spare_p, spare_v = sb("spare_p", [128, 8], F32), sb("spare_v", [128, 16], F32)
        minus_half = sb("minus_half", [128, CB], F32)
        xn = sb("xn", [128, CB, D], F32)
        xnt, cnt = sb("xnt", [128, CT], F32), sb("cnt", [128, CT], F32)
        qf, kf = sb("qf", [128, CT], F32), sb("kf", [128, CT], F32)
        q_hi, q_lo = sb("q_hi", [128, CB, T], F16), sb("q_lo", [128, CB, T], F16)
        k_hi, k_lo = sb("k_hi", [128, CB, T], F16), sb("k_lo", [128, CB, T], F16)
        q_st = sb("q_st", [128, 2, HQ, 4, T], F16)
        k_st = sb("k_st", [128, 2, 4, T], F16)
        v_st = sb("v_st", [128, CB, D], F32)
        v_s = sb("v_s", [128, CB, NH, VW], F32)
        negmax = sb("negmax", [128, 128], BF16)
        aug = sb("aug", [128, HQ, T], BF16)
        p_s = sb("p_s", [128, 2, UH * T], F32)
        rsum = sb("rsum", [128, NH], F32)
        o_n = sb("o_n", [128, NH, DK], F32)
        o_t = sb("o_t", [128, CB, T], F32)
        xn2 = sb("xn2", [128, CB, D], F32)
        x2tf = sb("x2tf", [128, CT], F32)
        esig = sb("esig", [128, CB, NE], F32)
        score, choice = sb("score", [128, CB, NE], F32), sb("choice", [128, CB, NE], F32)
        top_a, top_b = sb("top_a", [128, CB * NG, 4], F32), sb("top_b", [128, CB * NG, 4], F32)
        top_c, top_d = sb("top_c", [128, CB * NG, 4], F32), sb("top_d", [128, CB * NG, 4], F32)
        gscore = sb("gscore", [128, CB, NG], F32)
        cmp_a, cmp_b = sb("cmp_a", [128, CB, NG * NG], F32), sb("cmp_b", [128, CB, NG * NG], F32)
        gkeep = sb("gkeep", [128, CB, NG], F32)
        best = sb("best", [128, CB, TK], F32)
        rest = sb("rest", [128, CB, NE], F32)
        wsum = sb("wsum", [128, CB], F32)
        rw = sb("rw", [128, CB, NE], F32)
        rwcat = sb("rwcat", [128, CB, 2, NE], F16)

        sg, gu = p_s[:, :, 0:CT], p_s[:, :, CT:2 * CT]
        q_flat = q_st[:, :, :, :, :].rearrange("p a h j t -> p (a h j t)")
        h_f = q_flat[:, 0:4 * CT].bitcast(F32).rearrange("p (k n) -> p k n", k=2)
        h_parts = q_flat[:, 4 * CT:8 * CT].rearrange("p (a k n) -> p a k n", a=2, k=2)
        h_hi, h_lo = h_parts[:, 0], h_parts[:, 1]
        y_s, o_st = xnt, xn

        ps = ctx.enter_context(nc.psum_tensor("ps", [128, 8 * 512], F32))

        def bank(n, k=1):
            return ps[:, 512 * n:512 * (n + k)]

        s_const = sem("const_loaded")
        s_prep = sem("constants_prepared")
        s_x, s_c, s_m = sem("x_loaded"), sem("ctx_loaded"), sem("mask_loaded")
        s_w = [sem(f"weights_loaded_{k}") for k in range(WB)]
        s_oh = sem("onehot_loaded")
        s_sel = sem("selectors_loaded")
        s_whi = sem("weights_high")
        s_wsplit = sem("weights_split")
        s_xb = sem("residual_base_made")
        s_mb = sem("mask_bias_made")
        s_vc = sem("chain_vector")
        s_ac = sem("chain_scalar")
        s_pc = sem("chain_pool")
        s_var, s_rs = sem("x_variance"), sem("x_deviation")
        s_var2, s_rs2 = sem("x2_variance"), sem("x2_deviation")
        s_xn = sem("x_normalised")
        s_b6 = sem("bank6_read")
        s_xt, s_ct, s_qp, s_kp = sem("x_transposed"), sem("ctx_transposed"), sem("q_projected"), sem("k_projected")
        s_vp = sem("v_projected")
        s_xnt, s_cnt = sem("xnt_copied"), sem("cnt_copied")
        s_qf, s_kf = sem("q_copied"), sem("k_copied")
        s_qh, s_kh = sem("q_high"), sem("k_high")
        s_ql, s_kl = sem("q_low"), sem("k_low")
        s_ks, s_qs = sem("k_stack_selected"), sem("q_stack_selected")
        s_vst, s_v = sem("v_staged"), sem("v_ready")
        s_sc, s_max = sem("scores_ready"), sem("max_taken")
        s_mxt, s_aug = sem("max_transposed"), sem("aug_ready")
        s_sts, s_st = sem("key_scores_summed"), sem("exponents_ready")
        s_exp, s_pv = sem("probs_ready"), sem("pv_done")
        s_on, s_ot, s_otc = sem("heads_normalised"), sem("heads_transposed"), sem("heads_copied")
        s_wo, s_x2 = sem("attention_out"), sem("residual_added")
        s_xn2, s_x2t, s_x2f = sem("x2_normalised"), sem("x2_transposed"), sem("x2t_copied")
        s_x2h, s_x2l = sem("x2t_high"), sem("x2t_low")
        s_gl, s_es = sem("gate_logits"), sem("gate_exp")
        s_rw, s_rwt, s_rwc = sem("routing_ready"), sem("routing_transposed"), sem("routing_copied")
        s_g, s_u = sem("gate_ready"), sem("up_ready")
        s_rwe = sem("routing_expanded")
        s_sg, s_gup = sem("silu_ready"), sem("gate_times_up")
        s_h, s_hh, s_hl = sem("hidden_ready"), sem("hidden_high"), sem("hidden_low")
        s_d = sem("down_done")
        s_yc, s_yt, s_fin, s_out = sem("y_copied"), sem("y_transposed"), sem("output_made"), sem("output_stored")

        block = ctx.enter_context(nc.Block())

        USES = {
            "head": ["xt", "ct", "q", "k", "selk0", "selq0", "selk1"],
            "first": ["selq1", "selk2", "ct", "selq2", "xt", "ot0", "selk3", "q", "selq3", "ot1", "k",
                      "selk0", "selq0", "ot2", "selk1"],
            "inner": ["selq1", "ot3", "selk2", "ct", "selq2", "wo", "xt", "ot0", "selk3", "x2t", "q", "selq3", "gate",
                      "ot1", "k", "selk0", "selq0", "ot2", "selk1", "rwt"],
            "last": ["selq1", "ot3", "selk2", "selq2", "wo", "ot0", "selk3", "x2t", "selq3", "gate",
                     "ot1", "ot2", "rwt"],
            "tail": ["ot3", "wo", "x2t", "gate", "rwt"],
        }

        def before(c, use):
            if isinstance(c, str) and c == "head":
                kind, count = "head", 0
            elif isinstance(c, str):
                kind, count = "tail", before(NC - 1, "rwt") + 1
            elif isinstance(c, int) and c == 0:
                kind, count = "first", len(USES["head"])
            else:
                kind = "last" if isinstance(c, int) else "inner"
                count = len(USES["head"]) + len(USES["first"]) + (c - 1) * len(USES["inner"])
            return count + USES[kind].index(use)

        def after(c, use):
            return before(c, use) + 1

        @block.sync
        def _(sp):
            for dst, src in ((cst[:, :], consts), (wq_s[:, :], wq), (wk_s[:, :], wk), (wv_s[:, :], wv),
                             (wo_s[:, :], wo), (gw_s[:, :], gate_w), (bq_s[:, :], bq), (bk_s[:, :], bk)):
                sp.dma_start(dst, src).then_inc(s_const, 16)
            for dst, src in ((bv_s[:, :], bv), (bo_s[:, :], bo), (gb_s[:, :], gate_b)):
                sp.dma_start(dst, src.partition_broadcast(128)).then_inc(s_const, 16)
            sp.dma_start(x_in[:, :, :], x_v[0]).then_inc(s_x, 16)
            sp.dma_start(c_in[:, :, :], c_v[0]).then_inc(s_c, 16)
            sp.dma_start(m_in[:, :, :], m_v[0]).then_inc(s_m, 16)
            sp.dma_start(sel_s[:, :, :, :], sel).then_inc(s_sel, 16)
            sp.dma_start(onehot_s[:, :], onehot).then_inc(s_oh, 16)
            for k in range(WB):
                sp.dma_start(w_in[:, k, :], w_all[:, k * PC:(k + 1) * PC]).then_inc(s_w[k], 16)
            with sp.Fori(1, NP // WB) as turn:
                for k in range(WB):
                    piece = turn * WB + k
                    sp.wait_ge(s_wsplit, piece - WB + 1)
                    sp.dma_start(w_in[:, k, :], w_all[:, bass.ds(piece * PC, PC)]).then_inc(s_w[k], 16)
            for c in range(NC):
                sp.wait_ge(s_fin, c + 1)
                sp.dma_start(out_v[c], o_st[:, :, :]).then_inc(s_out, 16)
                sp.wait_ge(s_out, 16 * (c + 1))

        @block.gpsimd
        def _(pool):
            g = nc.gpsimd

            spare = {}

            def carry_wait(place):
                k = spare.setdefault(place, len(spare))
                g.tensor_tensor(spare_p[:, k:k + 1], minus_half[:, 0:1], minus_half[:, 1:2], ALU.add)

            g.memset(ones_b[:, :], 1.0).then_inc(s_prep, 1)
            g.memset(negmax[:, :], 0.0).then_inc(s_prep, 1)
            g.memset(v_s[:, :, :, :], 1.0).then_inc(s_prep, 1)
            g.memset(augmask[:, :, :], 1.0).then_inc(s_pc, 1)
            g.memset(minus_half[:, :], -0.5).then_inc(s_pc, 1)
            pool.wait_ge(s_const, 16 * 11)
            g.tensor_copy(ident_b[:, :], ident).then_inc(s_prep, 1)
            g.tensor_copy(ident_h[:, :], ident).then_inc(s_prep, 1)
            pool.wait_ge(s_pc, 2)
            for h in range(HQ):
                g.tensor_scalar(augmask[:, h, :], augmask[:, h, :], amask[:, h:h + 1], None, ALU.mult).then_inc(s_prep, 1)

            def prepare(c, lo, hi):
                carry_wait(("mask", lo))
                g.tensor_scalar(mbias[:, lo:hi, :], m_in[:, lo:hi, :], 0.0, MASKED,
                                ALU.is_equal, ALU.mult).then_inc(s_mb, 1)

            def base(c):
                bo_b = bo_s[:, :].unsqueeze(1).to_broadcast([128, CB, D])
                g.tensor_tensor(x2[:, bass.ds(c * CT, CT)].rearrange("p (b d) -> p b d", b=CB), x_in[:, :, :], bo_b,
                                ALU.add).then_inc(s_xb, 1)

            def v_copy(c):
                wait(pool, s_vst, c + 1)
                wait(pool, s_pv, NU * c)
                carry_wait("v")
                g.tensor_copy(v_s[:, :, :, 0:DK], v_st[:, :, :].rearrange("p b (h e) -> p b h e", h=NH))\
                    .then_inc(s_v, 1)

            def deviation(c):
                pool.wait_ge(s_var, c + 1)
                wait(pool, s_xn, c)
                g.tensor_tensor(rstd[:, :], var[:, :], minus_half[:, :], ALU.pow).then_inc(s_rs, 1)

            def deviation2(c):
                pool.wait_ge(s_var2, c + 1)
                wait(pool, s_xn2, c)
                g.tensor_tensor(rstd2[:, :], var2[:, :], minus_half[:, :], ALU.pow).then_inc(s_rs2, 1)

            pool.wait_ge(s_x, 16)
            deviation(0)
            base(0)
            pool.wait_ge(s_m, 16)
            prepare(0, 0, CB - 1)
            prepare(0, CB - 1, CB)
            pool.wait_ge(s_prep, 3)
            v_copy(0)

            def low_weights(c, u):
                piece = NU * (c - 1) + u
                pool.wait_ge(s_whi, piece + 1)
                at = bass.ds(piece * PC, PC)
                g.tensor_tensor(w_lo[:, at], w_in[:, u % WB, :], w_hi[:, at], ALU.subtract).then_inc(s_wsplit, 1)

            def chunk(c, inner):
                if inner:
                    low_weights(c, 0)
                pool.wait_ge(s_x, 16 * (c + 2))
                base(c + 1)
                deviation(c + 1)
                if inner:
                    low_weights(c, 1)
                    low_weights(c, 2)
                    deviation2(c - 1)
                    for u in range(3, NU):
                        low_weights(c, u)
                pool.wait_ge(s_m, 16 * (c + 2))
                pool.wait_ge(s_st, NU * c + 6)
                prepare(c + 1, 0, CB - 1)
                pool.wait_ge(s_st, NU * c + 8)
                prepare(c + 1, CB - 1, CB)
                v_copy(c + 1)

            chunk(0, False)
            with pool.Fori(1, NC - 1) as c:
                chunk(c, True)
            deviation2(NC - 2)
            deviation2(NC - 1)

            def low(n, k):
                pool.wait_ge(s_h, n + 1)
                pool.wait_ge(s_hh, n + 1)
                wait(pool, s_d, n - 1)
                g.tensor_tensor(h_lo[:, k % 2, :], h_f[:, k % 2, :], h_hi[:, k % 2, :], ALU.subtract).then_inc(s_hl, 1)

            def low_chunk(c):
                low(c * RB, 0)
                low(c * RB + 1, 1)
                with pool.Fori(0, RR // RU) as turn:
                    r = turn * RU
                    for k in range(RU):
                        low(c * RB + r + (RS + k), k)

            low_chunk(0)
            with pool.Fori(1, NC) as c:
                low_chunk(c)

        @block.scalar
        def _(act):
            a = nc.scalar

            def copy_xnt(c):
                wait(act, s_xt, c + 1)
                wait(act, s_qp, c)
                a.activation(xnt[:, :], bank(6), ACT.Copy).then_inc(s_b6, 1)

            def copy_cnt(c):
                wait(act, s_ct, c + 1)
                wait(act, s_kp, c)
                wait(act, s_vp, c)
                a.activation(cnt[:, :], bank(6), ACT.Copy).then_inc(s_b6, 1)

            def copy_q(c):
                wait(act, s_qp, c + 1)
                wait(act, s_ql, c)
                a.activation(qf[:, :], bank(6), ACT.Identity, bias=bq_s[:, 0:1]).then_inc(s_b6, 1)

            def copy_k(c):
                wait(act, s_kp, c + 1)
                wait(act, s_kl, c)
                a.activation(kf[:, :], bank(6), ACT.Identity, bias=bk_s[:, 0:1]).then_inc(s_b6, 1)

            def high_q(c, done):
                act.wait_ge(s_b6, done)
                wait(act, s_qs, CB * c)
                a.activation(q_hi[:, :, :].rearrange("p b t -> p (b t)"), qf[:, :], ACT.Copy).then_inc(s_qh, 1)

            def high_k(c, done):
                act.wait_ge(s_b6, done)
                wait(act, s_ks, CB * c)
                a.activation(k_hi[:, :, :].rearrange("p b t -> p (b t)"), kf[:, :], ACT.Copy).then_inc(s_kh, 1)

            def stack_k(c, b):
                n = CB * c + b
                wait(act, s_ks, n + 1)
                wait(act, s_sts, 2 * n - 2)
                a.activation(k_st[:, b % 2, :, :].rearrange("p j t -> p (j t)"), bank(6), ACT.Copy).then_inc(s_b6, 1)

            def stack_q(c, b):
                n = CB * c + b
                wait(act, s_qs, n + 1)
                wait(act, s_sts, 2 * n - 2)
                for h in range(HQ):
                    ins = a.activation(q_st[:, b % 2, h, :, :].rearrange("p j t -> p (j t)"), bank(6), ACT.Copy,
                                       scale=qmask[:, h:h + 1])
                ins.then_inc(s_b6, 1)

            def high_weights(c, u):
                piece = NU * (c - 1) + u
                act.wait_ge(s_w[u % WB], 16 * ((c - 1) * (NU // WB) + (u // WB + 1)))
                a.activation(w_hi[:, bass.ds(piece * PC, PC)], w_in[:, u % WB, :], ACT.Copy).then_inc(s_whi, 1)

            def loads(c):
                act.wait_ge(s_xn, c)
                act.wait_ge(s_xb, c)
                act.dma_start(x_in[:, :, :], x_v[bass.ds(c, 1)].squeeze(0)).then_inc(s_x, 16)
                act.wait_ge(s_ct, c)
                act.dma_start(c_in[:, :, :], c_v[bass.ds(c, 1)].squeeze(0)).then_inc(s_c, 16)
                act.wait_ge(s_mb, 2 * c)
                act.dma_start(m_in[:, :, :], m_v[bass.ds(c, 1)].squeeze(0)).then_inc(s_m, 16)

            def exp(c, u):
                n = NU * c + u
                wait(act, s_st, n + 1)
                wait(act, s_pv, n - 1)
                a.activation(p_s[:, u % 2, :], bank(2 + 2 * (u % 2), 2), ACT.Exp, scale=DK ** -0.5).then_inc(s_exp, 1)

            def copy_ot(c, b):
                wait(act, s_ot, CB * c + b + 1)
                wait(act, s_wo, c)
                a.activation(o_t[:, b, :], bank(6)[:, 0:T], ACT.Copy).then_inc(s_b6, 1)

            def copy_x2t(c, done):
                wait(act, s_x2t, c + 1)
                wait(act, s_gl, c)
                wait(act, s_x2l, c)
                a.activation(x2tf[:, :], bank(6), ACT.Copy).then_inc(s_b6, 1)
                wait(act, s_b6, done)
                a.activation(x2t_hi[:, bass.ds(c * CT, CT)], x2tf[:, :], ACT.Copy).then_inc(s_x2h, 1)

            def exp_gate(c):
                wait(act, s_gl, c + 1)
                wait(act, s_rw, c)
                a.activation(esig[:, :, :].rearrange("p b e -> p (b e)"), bank(6)[:, 0:CB * NE], ACT.Exp,
                             scale=-1.0).then_inc(s_b6, 1)

            def copy_rwt(c):
                wait(act, s_rwt, c + 1)
                src = bank(6)[:, 0:CT // 2].bitcast(F16)
                a.activation(rwt[:, bass.ds(c * CT, CT)], src, ACT.Copy).then_inc(s_b6, 1)

            act.wait_ge(s_const, 16 * 11)
            copy_xnt(0)
            copy_cnt(0)
            copy_q(0)
            copy_k(0)
            high_q(0, after("head", "q"))
            high_k(0, after("head", "k"))
            stack_k(0, 0)
            stack_q(0, 0)
            stack_k(0, 1)

            def chunk(c, prev, nxt):
                inner = prev and nxt
                for u in range(NU):
                    b = u // 2
                    if u == 0 and nxt:
                        loads(c + 1)
                    if u == 1 and prev:
                        copy_ot(c - 1, CB - 1)
                    if u == 2 and nxt:
                        copy_cnt(c + 1)
                    if u in (3, 5, 7):
                        copy_ot(c, b - 1)
                    if u == 4 and nxt:
                        copy_q(c + 1)
                    if u == 6 and nxt:
                        stack_k(c + 1, 0)
                    exp(c, u)
                    if inner:
                        high_weights(c, u)
                    if u in (1, 3):
                        stack_k(c, b + 2)
                    elif u == 7 and nxt:
                        stack_k(c + 1, 1)
                    elif u in (0, 2, 4):
                        stack_q(c, b + 1)
                    elif u == 6 and nxt:
                        stack_q(c + 1, 0)
                    if u == 2 and nxt:
                        copy_xnt(c + 1)
                    if u == 3 and prev:
                        copy_x2t(c - 1, after(c, "x2t"))
                    if u == 4 and prev:
                        exp_gate(c - 1)
                    if u == 5 and nxt:
                        copy_k(c + 1)
                        high_k(c + 1, after(c, "k"))
                        high_q(c + 1, after(c, "q"))
                    if u == 7 and prev:
                        copy_rwt(c - 1)

            chunk(0, False, True)
            with act.Fori(1, NC - 1) as c:
                chunk(c, True, True)
            chunk(NC - 1, True, False)
            copy_ot(NC - 1, 3)
            copy_x2t(NC - 1, after("tail", "x2t"))
            exp_gate(NC - 1)
            copy_rwt(NC - 1)

            def silu(n, k):
                act.wait_ge(s_g, n + 1)
                wait(act, s_gup, n - 1)
                a.activation(sg[:, k % 2, :], bank(k % 2), ACT.Silu).then_inc(s_sg, 1)

            def high(n, k):
                act.wait_ge(s_h, n + 1)
                wait(act, s_d, n - 1)
                a.activation(h_hi[:, k % 2, :], h_f[:, k % 2, :], ACT.Copy).then_inc(s_hh, 1)

            def y_copy(c):
                wait(act, s_d, RB * (c + 1))
                wait(act, s_yt, c)
                a.activation(y_s[:, :], bank(6), ACT.Copy).then_inc(s_yc, 1)

            def ffn_chunk(c, prev):
                silu(c * RB, 0)
                if prev:
                    high(c * RB - 1, 1)
                silu(c * RB + 1, 1)
                high(c * RB, 0)
                if prev:
                    y_copy(c - 1)
                with act.Fori(0, RR // RU) as turn:
                    r = turn * RU
                    for k in range(RU):
                        n = c * RB + r + (RS + k)
                        silu(n, k)
                        high(n - 1, k + 1)

            ffn_chunk(0, False)
            with act.Fori(1, NC) as c:
                ffn_chunk(c, True)
            high(NC * RB - 1, 1)
            y_copy(NC - 1)

        @block.vector
        def _(dve):
            v = nc.vector

            spare = {}

            def carry_wait(place):
                k = spare.setdefault(place, len(spare))
                v.memset(spare_v[:, k:k + 1], 0.0)

            state = {"base": 0, "k": 0}

            def link(ins):
                ins.then_inc(s_vc, 1)
                state["k"] += 1
                dve.wait_ge(s_vc, state["base"] + state["k"])

            def moments(src, mv_, var_, signal):
                carry_wait(("stats", mv_ is mv))
                for b in range(CB):
                    ins = v.bn_stats(stats[:, b, :], src(b))
                link(ins)
                carry_wait(("aggregate", mv_ is mv))
                for b in range(CB):
                    ins = v.bn_aggr(mv_[:, b, :], stats[:, b, :])
                link(ins)
                v.tensor_scalar(var_[:, :], mv_[:, :, 1], EPS, None, ALU.add).then_inc(signal, 1)

            def normalise(dst, src, mv_, rstd_, signal):
                for b in range(CB):
                    ins = v.tensor_scalar(dst[:, b, :], src(b), mv_[:, b, 0:1], rstd_[:, b:b + 1],
                                          ALU.subtract, ALU.mult)
                ins.then_inc(signal, 1)

            def x_moments(c):
                wait(dve, s_x, 16 * (c + 1))
                wait(dve, s_rs, c)
                moments(lambda b: x_in[:, b, :], mv, var, s_var)

            def norm_x(c):
                wait(dve, s_rs, c + 1)
                wait(dve, s_xt, c)
                normalise(xn, lambda b: x_in[:, b, :], mv, rstd, s_xn)

            def low_parts(c):
                for high, low, full, ready, signal in ((k_hi, k_lo, kf, s_kh, s_kl), (q_hi, q_lo, qf, s_qh, s_ql)):
                    wait(dve, ready, c + 1)
                    v.tensor_tensor(low[:, :, :].rearrange("p b t -> p (b t)"), full[:, :],
                                    high[:, :, :].rearrange("p b t -> p (b t)"), ALU.subtract).then_inc(signal, 1)

            def v_stage(c):
                wait(dve, s_vp, c + 1)
                wait(dve, s_v, c)
                v.tensor_tensor(v_st[:, :, :], bank(0).rearrange("p (b d) -> p b d", b=CB),
                                bv_s[:, :].unsqueeze(1).to_broadcast([128, CB, D]), ALU.add).then_inc(s_vst, 1)

            def row_max(c, u):
                n = NU * c + u
                half = u % 2
                wait(dve, s_sc, n + 1)
                wait(dve, s_mxt, n - 1)
                dst = negmax[:, 64 * half:64 * half + 64].rearrange("p (j q) -> p j q", j=2)[:, :, 0:HQ]
                v.tensor_reduce(dst, bank(0, 2).rearrange("p (j h s) -> p j h s", j=2, h=HQ), AX.X, ALU.max,
                                negate=True).then_inc(s_max, 1)

            def aug_rows(c, u):
                n = NU * c + u
                p0 = 64 * (u % 2)
                wait(dve, s_mxt, n + 1)
                wait(dve, s_st, n - 1)
                v.tensor_tensor(aug[p0:p0 + 64, :, :],
                                bank(7)[p0:p0 + 64, 0:T].unsqueeze(1).to_broadcast([64, HQ, T]),
                                augmask[p0:p0 + 64, :, :], ALU.mult).then_inc(s_aug, 1)

            def norm_heads(c, b):
                wait(dve, s_pv, NU * c + 2 * b + 2)
                wait(dve, s_ot, CB * c + b)
                o = bank(7)[:, 256:256 + NH * VW].rearrange("p (h e) -> p h e", e=VW)
                link(v.reciprocal(rsum[:, :], o[:, :, DK]))
                v.tensor_tensor(o_n[:, :, :], o[:, :, 0:DK], rsum[:, :].unsqueeze(2).to_broadcast([128, NH, DK]),
                                ALU.mult).then_inc(s_on, 1)

            def x2_chunk(c):
                return x2[:, bass.ds(c * CT, CT)]

            def residual(c):
                wait(dve, s_wo, c + 1)
                v.tensor_tensor(x2_chunk(c), x2_chunk(c), bank(6), ALU.add).then_inc(s_b6, 1)

            def x2_moments(c, done):
                dve.wait_ge(s_b6, done)
                wait(dve, s_rs2, c)
                moments(lambda b: x2[:, bass.ds(c * CT + b * D, D)], mv2, var2, s_var2)

            def norm_x2(c):
                wait(dve, s_rs2, c + 1)
                wait(dve, s_x2t, c)
                normalise(xn2, lambda b: x2[:, bass.ds(c * CT + b * D, D)], mv2, rstd2, s_xn2)

            def x2t_low(c):
                wait(dve, s_x2h, c + 1)
                v.tensor_tensor(x2t_lo[:, bass.ds(c * CT, CT)], x2tf[:, :], x2t_hi[:, bass.ds(c * CT, CT)],
                                ALU.subtract).then_inc(s_x2l, 1)

            flat = "p b e -> p (b e)"
            quad = "p b (i j) -> p b i j"

            def group_scores(c, done):
                dve.wait_ge(s_b6, done)
                wait(dve, s_rwt, c)
                link(v.tensor_scalar(esig[:, :, :], esig[:, :, :], 1.0, None, ALU.add))
                link(v.reciprocal(score[:, :, :].rearrange(flat), esig[:, :, :].rearrange(flat)))
                link(v.tensor_tensor(choice[:, :, :], score[:, :, :],
                                     gb_s[:, :].unsqueeze(1).to_broadcast([128, CB, NE]), ALU.add))
                m = choice[:, :, :].rearrange(flat).rearrange("p (g e) -> p g e", e=GE)
                v.tensor_tensor(top_a[:, :, :], m[:, :, 0:4], m[:, :, 4:8], ALU.max)
                link(v.tensor_tensor(top_b[:, :, :], m[:, :, 0:4], m[:, :, 4:8], ALU.min))
                a_, b_, c_, d_ = top_a, top_b, top_c, top_d
                for w in (2, 1):
                    v.tensor_tensor(c_[:, :, 0:w], a_[:, :, 0:w], a_[:, :, w:2 * w], ALU.max)
                    v.tensor_tensor(d_[:, :, 0:w], a_[:, :, 0:w], a_[:, :, w:2 * w], ALU.min)
                    link(v.tensor_tensor(d_[:, :, 2:2 + w], b_[:, :, 0:w], b_[:, :, w:2 * w], ALU.max))
                    link(v.tensor_tensor(d_[:, :, 0:w], d_[:, :, 0:w], d_[:, :, 2:2 + w], ALU.max))
                    a_, b_, c_, d_ = c_, d_, a_, b_
                link(v.tensor_tensor(gscore[:, :, :].rearrange("p b g -> p (b g)"), a_[:, :, 0], b_[:, :, 0], ALU.add))

            def keep_groups():
                other = gscore[:, :, :].unsqueeze(2).to_broadcast([128, CB, NG, NG])
                own = gscore[:, :, :].unsqueeze(3).to_broadcast([128, CB, NG, NG])
                v.tensor_tensor(cmp_a[:, :, :].rearrange(quad, i=NG), other, own, ALU.is_gt)
                link(v.tensor_tensor(cmp_b[:, :, :].rearrange(quad, i=NG), other, own, ALU.is_ge))
                link(v.tensor_tensor(cmp_b[:, :, :], cmp_b[:, :, :], tri.unsqueeze(1).to_broadcast([128, CB, NG * NG]),
                                     ALU.mult))
                link(v.tensor_tensor(cmp_a[:, :, :], cmp_a[:, :, :], cmp_b[:, :, :], ALU.max))
                link(v.tensor_reduce(gkeep[:, :, :], cmp_a[:, :, :].rearrange(quad, i=NG), AX.X, ALU.add))
                link(v.tensor_scalar(gkeep[:, :, :], gkeep[:, :, :], float(GK), None, ALU.is_lt))
                link(v.tensor_tensor(choice[:, :, :].rearrange("p b (g e) -> p b g e", e=GE),
                                     choice[:, :, :].rearrange("p b (g e) -> p b g e", e=GE),
                                     gkeep[:, :, :].unsqueeze(3).to_broadcast([128, CB, NG, GE]), ALU.mult))

            def weigh_experts():
                carry_wait("best")
                for b in range(CB):
                    ins = v.max(best[:, b, :], choice[:, b, :])
                link(ins)
                carry_wait("rest")
                for b in range(CB):
                    ins = v.match_replace(rest[:, b, :], best[:, b, :], choice[:, b, :], PICKED)
                link(ins)
                link(v.scalar_tensor_tensor(rw[:, :, :].rearrange(flat), rest[:, :, :].rearrange(flat), PICKED,
                                            score[:, :, :].rearrange(flat), ALU.is_equal, ALU.mult))
                link(v.tensor_reduce(wsum[:, :], rw[:, :, :], AX.X, ALU.add))
                link(v.tensor_scalar(wsum[:, :], wsum[:, :], 1e-20, None, ALU.add))
                link(v.reciprocal(wsum[:, :], wsum[:, :]))
                link(v.scalar_tensor_tensor(rw[:, :, :], rw[:, :, :], ROUTED_SCALE,
                                            wsum[:, :].unsqueeze(2).to_broadcast([128, CB, NE]), ALU.mult, ALU.mult))
                link(v.tensor_copy(rwcat[:, :, 0, :], rw[:, :, :]))
                v.tensor_tensor(rwcat[:, :, 1, :], rw[:, :, :], rwcat[:, :, 0, :], ALU.subtract).then_inc(s_rw, 1)

            dve.wait_ge(s_const, 16 * 11)
            dve.wait_ge(s_prep, 9)
            x_moments(0)
            norm_x(0)
            low_parts(0)
            v_stage(0)

            def chunk(c, prev, nxt):
                row_max(c, 0)
                for u in range(NU):
                    if u == 2 and nxt:
                        norm_x(c + 1)
                    if u == 3 and prev:
                        norm_x2(c - 1)
                    aug_rows(c, u)
                    if u + 1 < NU:
                        row_max(c, u + 1)
                    if u % 2 == 0:
                        if u:
                            norm_heads(c, u // 2 - 1)
                        elif prev:
                            norm_heads(c - 1, CB - 1)
                    if u == 1 and nxt:
                        x_moments(c + 1)
                    if u == 2 and prev:
                        residual(c - 1)
                        x2_moments(c - 1, after(c, "wo"))
                    if u == 3 and prev:
                        x2t_low(c - 1)
                    if u == 4 and prev:
                        group_scores(c - 1, after(c, "gate"))
                    if u == 5 and prev:
                        keep_groups()
                    if u == 6 and prev:
                        weigh_experts()
                    if u == 5 and nxt:
                        low_parts(c + 1)
                    if u == 7 and nxt:
                        v_stage(c + 1)

            chunk(0, False, True)
            assert state["k"] == CHAIN_FIRST, state["k"]
            state["k"] = 0
            with dve.Fori(1, NC - 1) as c:
                state["base"] = CHAIN_FIRST + (c - 1) * CHAIN_INNER
                chunk(c, True, True)
            assert state["k"] == CHAIN_INNER, state["k"]
            state.update(base=CHAIN_FIRST + (NC - 2) * CHAIN_INNER, k=0)
            chunk(NC - 1, True, False)
            norm_heads(NC - 1, CB - 1)
            residual(NC - 1)
            x2_moments(NC - 1, after("tail", "wo"))
            norm_x2(NC - 1)
            x2t_low(NC - 1)
            group_scores(NC - 1, after("tail", "gate"))
            keep_groups()
            weigh_experts()

            def gate_up(n, k):
                dve.wait_ge(s_sg, n + 1)
                dve.wait_ge(s_u, n + 1)
                v.tensor_tensor(gu[:, k % 2, :], sg[:, k % 2, :], bank(2 + k % 2), ALU.mult).then_inc(s_gup, 1)

            def hidden(n, k, routed):
                wait(dve, s_gup, n + 1)
                wait(dve, s_hl, n - 1)
                if routed is None:
                    v.tensor_copy(h_f[:, k % 2, :], gu[:, k % 2, :]).then_inc(s_h, 1)
                else:
                    dve.wait_ge(s_rwe, routed + 1)
                    v.tensor_tensor(h_f[:, k % 2, :], gu[:, k % 2, :], bank(4 + k % 2), ALU.mult).then_inc(s_h, 1)

            def output(c):
                wait(dve, s_yt, c + 1)
                wait(dve, s_out, 16 * c)
                v.tensor_tensor(o_st[:, :, :].rearrange("p b d -> p (b d)"), x2_chunk(c), bank(7),
                                ALU.add).then_inc(s_fin, 1)

            def ffn_chunk(c, prev):
                for k in range(RS):
                    gate_up(c * RB + k, k)
                    hidden(c * RB + k, k, None)
                with dve.Fori(0, RR // RU) as turn:
                    r = turn * RU
                    for k in range(RU):
                        gate_up(c * RB + r + (RS + k), k)
                        hidden(c * RB + r + (RS + k), k, c * RR + r + k)
                if prev:
                    output(c - 1)

            ffn_chunk(0, False)
            with dve.Fori(1, NC) as c:
                ffn_chunk(c, True)
            output(NC - 1)

        @block.tensor
        def _(pe):
            t = nc.tensor

            def heads4(ap):
                return ap.rearrange("p (h t) -> p h t", h=HQ)

            def transpose4(src, done, signal):
                pe.wait_ge(s_b6, done) if not isinstance(done, int) or done > 0 else None
                for b in range(CB):
                    ins = t.transpose(bank(6)[:, b * 128:(b + 1) * 128], src(b), ident)
                ins.then_inc(signal, 1)

            def x_transpose(c, done):
                wait(pe, s_xn, c + 1)
                transpose4(lambda b: xn[:, b, :], done, s_xt)

            def ctx_transpose(c, done):
                wait(pe, s_c, 16 * (c + 1))
                transpose4(lambda b: c_in[:, b, :], done, s_ct)

            def project(w, src, done, signal):
                wait(pe, s_b6, done)
                t.matmul(bank(6), w[:, :], src[:, :], start=True, stop=True).then_inc(signal, 1)

            def project_v(c, done):
                wait(pe, s_b6, done)
                wait(pe, s_max, NU * c)
                for b in range(CB):
                    ins = t.matmul(bank(0)[:, b * 128:(b + 1) * 128], cnt[:, b * 128:(b + 1) * 128], wv_s[:, :],
                                   start=True, stop=True)
                ins.then_inc(s_vp, 1)

            def pair(u):
                return [(jj, 2 * (u % 2) + jj) for jj in range(2)]

            def select(c, b, done, parts, selectors, ready, signal):
                wait(pe, ready, c + 1)
                wait(pe, s_b6, done)
                for j in range(4):
                    t.matmul(bank(6)[:, j * T:(j + 1) * T], selectors[0][:, j, :], parts[0][:, b, :],
                             start=True, stop=False)
                    ins = t.matmul(bank(6)[:, j * T:(j + 1) * T], selectors[1][:, j, :], parts[1][:, b, :],
                                   start=False, stop=True)
                ins.then_inc(signal, 1)

            def select_k(c, b, done):
                select(c, b, done, (k_hi, k_lo), k_sel, s_kl, s_ks)

            def select_q(c, b, done):
                select(c, b, done, (q_hi, q_lo), q_sel, s_ql, s_qs)

            def scores(c, u, stacked):
                n, b = NU * c + u, u // 2
                wait(pe, s_max, n)
                if u == 0:
                    wait(pe, s_vst, c + 1)
                wait(pe, s_b6, stacked)
                for jj, j in pair(u):
                    for h in range(HQ):
                        t.matmul(bank(jj)[:, h * T:(h + 1) * T], q_st[:, b % 2, h, j, :], k_st[:, b % 2, j, :],
                                 start=True, stop=False, skip_group_check=True)
                wait(pe, s_mb, 2 * c + (1 if b < CB - 1 else 2))
                for jj, j in pair(u):
                    ins = t.matmul(heads4(bank(jj)), ident_b[:, :],
                                   mbias[:, b, :].unsqueeze(1).to_broadcast([128, HQ, T]), start=False, stop=True,
                                   skip_group_check=True)
                ins.then_inc(s_sc, 1)

            def key_scores(c, u):
                n, b, first = NU * c + u, u // 2, 2 + 2 * (u % 2)
                wait(pe, s_exp, n - 1)
                for jj, j in pair(u):
                    ins = t.matmul(heads4(bank(first + jj)), k_st[:, b % 2, j, :], q_st[:, b % 2, :, j, :],
                                   start=True, stop=False)
                ins.then_inc(s_sts, 1)

            def max_transpose(c, u):
                p0 = 64 * (u % 2)
                wait(pe, s_max, NU * c + u + 1)
                if u % 2:
                    wait(pe, s_on, CB * c + (u - 1) // 2)
                t.matmul(bank(7)[p0:p0 + 64, 0:T], negmax[:, p0:p0 + 64], ident_b[:, :],
                         start=True, stop=True).then_inc(s_mxt, 1)

            def mask_and_max(c, u):
                n, b, first = NU * c + u, u // 2, 2 + 2 * (u % 2)
                for jj, j in pair(u):
                    t.matmul(heads4(bank(first + jj)), mbias[:, b, :],
                             ident_b[:, :].unsqueeze(1).to_broadcast([128, HQ, T]), start=False, stop=False)
                wait(pe, s_aug, n + 1)
                for jj, j in pair(u):
                    q = slice(32 * j, 32 * j + 32)
                    ins = t.matmul(heads4(bank(first + jj)), ones_b[q, :], aug[q, :, :], start=False, stop=True)
                ins.then_inc(s_st, 1)

            def attend(c, u):
                n, b = NU * c + u, u // 2
                wait(pe, s_exp, n + 1)
                if u == 0:
                    wait(pe, s_v, c + 1)
                for hh in range(UH):
                    h = UH * (u % 2) + hh
                    ins = t.matmul(bank(7)[:, 256 + h * VW:256 + (h + 1) * VW], p_s[:, u % 2, hh * T:(hh + 1) * T],
                                   v_s[:, b, h, :], start=True, stop=True)
                ins.then_inc(s_pv, 1)

            def out_transpose(c, b, done):
                wait(pe, s_on, CB * c + b + 1)
                wait(pe, s_b6, done)
                t.transpose(bank(6)[:, 0:128], o_n[:, :, :].rearrange("p h e -> p (h e)"), ident).then_inc(s_ot, 1)

            def attention_out(done):
                wait(pe, s_b6, done)
                for b in range(CB):
                    ins = t.matmul(bank(6)[:, b * 128:(b + 1) * 128], o_t[:, b, :], wo_s[:, :], start=True, stop=True)
                ins.then_inc(s_wo, 1)

            def x2_transpose(c, done):
                wait(pe, s_xn2, c + 1)
                transpose4(lambda b: xn2[:, b, :], done, s_x2t)

            def gate(done):
                wait(pe, s_b6, done)
                for b in range(CB):
                    ins = t.matmul(bank(6)[:, b * NE:(b + 1) * NE], x2tf[:, b * 128:(b + 1) * 128], gw_s[:, :],
                                   start=True, stop=True)
                ins.then_inc(s_gl, 1)

            def routing_transpose(c, done):
                wait(pe, s_rw, c + 1)
                wait(pe, s_b6, done)
                for b in range(CB):
                    ins = t.transpose(bank(6)[:, 64 * b:64 * b + 64].bitcast(F16),
                                      rwcat[:, b, :, :].rearrange("p k e -> p (k e)"), ident_h[:, :])
                ins.then_inc(s_rwt, 1)

            pe.wait_ge(s_const, 16 * 11)
            pe.wait_ge(s_prep, 9)
            x_transpose(0, 0)
            ctx_transpose(0, 1)
            project(wq_s, xnt, 2, s_qp)
            project(wk_s, cnt, 3, s_kp)
            project_v(0, after("head", "ct"))
            pe.wait_ge(s_sel, 16)
            select_k(0, 0, before("head", "selk0"))
            select_q(0, 0, before("head", "selq0"))
            select_k(0, 1, before("head", "selk1"))

            def chunk(c, prev, nxt):
                def at(use):
                    return before(c, use)

                def stacked(b):
                    if b:
                        return after(c, f"selq{b}")
                    return at("selq1") - (2 if prev else 1)

                scores(c, 0, stacked(0))
                for u in range(NU):
                    b = u // 2
                    key_scores(c, u)
                    max_transpose(c, u)
                    if u == 1 and prev:
                        out_transpose(c - 1, CB - 1, at("ot3"))
                    if u == 2 and nxt:
                        ctx_transpose(c + 1, at("ct"))
                    if u in (3, 5, 7):
                        out_transpose(c, b - 1, at(f"ot{b - 1}"))
                    if u == 4 and nxt:
                        project(wq_s, xnt, at("q"), s_qp)
                    if u + 1 < NU:
                        scores(c, u + 1, stacked((u + 1) // 2))
                    if u == 6 and nxt:
                        select_k(c + 1, 0, at("selk0"))
                    mask_and_max(c, u)
                    if u in (1, 3):
                        select_k(c, b + 2, at(f"selk{b + 2}"))
                    elif u == 7 and nxt:
                        select_k(c + 1, 1, at("selk1"))
                    elif u in (0, 2, 4):
                        select_q(c, b + 1, at(f"selq{b + 1}"))
                    elif u == 6 and nxt:
                        select_q(c + 1, 0, at("selq0"))
                    if u:
                        attend(c, u - 1)
                    elif prev:
                        attend(c - 1, NU - 1)
                    if u == 2 and prev:
                        attention_out(at("wo"))
                    if u == 2 and nxt:
                        x_transpose(c + 1, at("xt"))
                    if u == 3 and prev:
                        x2_transpose(c - 1, at("x2t"))
                    if u == 4 and prev:
                        gate(at("gate"))
                    if u == 5 and nxt:
                        project(wk_s, cnt, at("k"), s_kp)
                    if u == 7 and nxt:
                        project_v(c + 1, at("k"))
                    if u == 7 and prev:
                        routing_transpose(c - 1, at("rwt"))

            chunk(0, False, True)
            with pe.Fori(1, NC - 1) as c:
                chunk(c, True, True)
            chunk(NC - 1, True, False)
            attend(NC - 1, NU - 1)
            out_transpose(NC - 1, CB - 1, before("tail", "ot3"))
            attention_out(before("tail", "wo"))
            x2_transpose(NC - 1, before("tail", "x2t"))
            gate(before("tail", "gate"))
            routing_transpose(NC - 1, before("tail", "rwt"))

            pe.wait_ge(s_exp, NC * NU)
            pe.wait_ge(s_b6, after("tail", "rwt"))
            pe.wait_ge(s_x2l, NC)
            pe.wait_ge(s_wsplit, NP)
            pe.wait_ge(s_oh, 16)

            def split_product(out, w_at, a, b, start, stop):
                t.matmul(out, w_hi[:, w_at], a, start=start, stop=False)
                t.matmul(out, w_hi[:, w_at], b, start=False, stop=False)
                return t.matmul(out, w_lo[:, w_at], a, start=False, stop=stop)

            def gate_and_up(n, c, k, block):
                wait(pe, s_sg, n - 1)
                wait(pe, s_gup, n - 1)
                tok = bass.ds(c * CT, CT)
                a, b = x2t_hi[:, tok], x2t_lo[:, tok]
                split_product(bank(k % 2), bass.ds(block * 128, 128), a, b, True, True).then_inc(s_g, 1)
                split_product(bank(2 + k % 2), bass.ds(WC + block * 128, 128), a, b, True, True).then_inc(s_u, 1)

            def expand(n, c, k, block):
                wait(pe, s_h, n - 1)
                t.matmul(bank(4 + k % 2), onehot_s[:, bass.ds(block * 128, 128)], rwt[:, bass.ds(c * CT, CT)],
                         start=True, stop=True).then_inc(s_rwe, 1)

            def down(n, k, block, start=False, stop=False):
                wait(pe, s_hl, n + 1)
                split_product(bank(6), bass.ds(2 * WC + block * 128, 128), h_hi[:, k % 2, :], h_lo[:, k % 2, :],
                              start, stop).then_inc(s_d, 1)

            def y_transpose(c):
                wait(pe, s_yc, c + 1)
                wait(pe, s_fin, c)
                for b in range(CB):
                    ins = t.transpose(bank(7)[:, b * 128:(b + 1) * 128], y_s[:, b * 128:(b + 1) * 128], ident)
                ins.then_inc(s_yt, 1)

            def ffn_chunk(c, prev):
                n = c * RB
                for k in range(RS):
                    gate_and_up(n + k, c, k, RR + k)
                    if prev:
                        down(n + k - 2, k, RR - 2 + k, stop=k == 1)
                for k in range(RU):
                    gate_and_up(n + RS + k, c, k, k)
                    expand(n + RS + k, c, k, k)
                    if k == 0:
                        wait(pe, s_yc, c)
                    down(n + k, k, RR + k if k < RS else k - RS, start=k == 0)
                with pe.Fori(1, RR // RU) as turn:
                    r = turn * RU
                    for k in range(RU):
                        gate_and_up(n + r + (RS + k), c, k, r + k)
                        expand(n + r + (RS + k), c, k, r + k)
                        down(n + r + k, k, r + (k - RS))
                if prev:
                    y_transpose(c - 1)

            ffn_chunk(0, False)
            with pe.Fori(1, NC) as c:
                ffn_chunk(c, True)
            for k in range(2):
                down(NC * RB - 2 + k, k, RR - 2 + k, stop=k == 1)
            y_transpose(NC - 1)


def kernel(x, ctx_1024, mask_BxSxS2_ik1, L0_xattn_Wq, L0_xattn_bq, L0_xattn_Wk, L0_xattn_bk, L0_xattn_Wv,
           L0_xattn_bv, L0_xattn_Wo, L0_xattn_bo, L0_ffn_gate_w, L0_ffn_gate_bias, L0_ffn_Wg, L0_ffn_Wu,
           L0_ffn_Wd, L0_ffn_Sg, L0_ffn_Su, L0_ffn_Sd):
    import concourse.bacc as bacc
    from concourse.bass_utils import run_bass_kernel_spmd

    a = np.ascontiguousarray
    pad = np.zeros((WC - NE * EI - SI, D), np.float32)
    rows_g = np.concatenate([np.asarray(L0_ffn_Wg).reshape(NE * EI, D), np.asarray(L0_ffn_Sg), pad])
    rows_u = np.concatenate([np.asarray(L0_ffn_Wu).reshape(NE * EI, D), np.asarray(L0_ffn_Su), pad])
    rows_d = np.concatenate([np.asarray(L0_ffn_Wd).transpose(0, 2, 1).reshape(NE * EI, D), np.asarray(L0_ffn_Sd).T, pad])
    w_all = np.concatenate([rows_g.T, rows_u.T, rows_d.reshape(RB, 128, D).transpose(1, 0, 2).reshape(128, RB * D)], 1)

    p = np.arange(128)[:, None]
    g = np.arange(HQ)[None, :]
    own, other = np.divmod(np.arange(NG * NG)[None, :], NG)
    consts = np.concatenate([np.eye(128), (p % 32) // DK == g, p % 32 == g, np.broadcast_to(other < own, (128, NG * NG))],
                            1).astype(np.float32)
    part, row, j, col = np.ogrid[0:4, 0:128, 0:4, 0:128]
    takes = np.array([[1, 0, 1, 0], [0, 1, 0, 0], [1, 1, 0, 0], [0, 0, 1, 0]])
    sel = ((row == 32 * j + col % 32) & (takes[part, col // 32] == 1)).transpose(1, 0, 2, 3).astype(np.float16)
    onehot = (p % NE == np.arange(RR * 128)[None, :] // EI).astype(np.float16)

    arrays = {
        "x": np.asarray(x), "ctx": np.asarray(ctx_1024), "mask": np.asarray(mask_BxSxS2_ik1),
        "wq": np.asarray(L0_xattn_Wq).T, "wk": np.asarray(L0_xattn_Wk).T,
        "wv": np.asarray(L0_xattn_Wv).T, "wo": np.asarray(L0_xattn_Wo).T,
        "bq": np.asarray(L0_xattn_bq).reshape(D, 1), "bk": np.asarray(L0_xattn_bk).reshape(D, 1),
        "bv": np.asarray(L0_xattn_bv), "bo": np.asarray(L0_xattn_bo),
        "gate_w": np.asarray(L0_ffn_gate_w).T, "gate_b": np.asarray(L0_ffn_gate_bias),
        "w_all": w_all, "consts": consts, "sel": sel, "onehot": onehot,
    }
    arrays = {k + "_dram": a(v) for k, v in arrays.items()}
    nc = bacc.Bacc("TRN2", target_bir_lowering=False, num_devices=1)
    args = [nc.dram_tensor(k, v.shape, mybir.dt.from_np(v.dtype), kind="ExternalInput").ap() for k, v in arrays.items()]
    args.append(nc.dram_tensor("out_dram", (B, T, D), F32, kind="ExternalOutput").ap())
    build(nc, *args)
    r = run_bass_kernel_spmd(nc, [arrays], core_ids=[0])
    return r.results[0]["out_dram"]
```

```python
import numpy as np
import concourse.bass as bass
from concourse import mybir
from contextlib import ExitStack

F32, F16, BF16, I32 = mybir.dt.float32, mybir.dt.float16, mybir.dt.bfloat16, mybir.dt.int32
ALU = mybir.AluOpType
ACT = mybir.ActivationFunctionType
AX = mybir.AxisListType

B, T, D = 32, 128, 128
NH, DK = 16, 8
NE, EI, SI = 64, 88, 176
NG, GE, GK, TK = 8, 8, 4, 8
CB = 4
NC = B // CB
CT = CB * T
HQ = 4
UH = 8
NU = CB * NH // UH
VW = DK + 1
RR = NE * EI // 128
RS = -(-SI // 128)
RB = RR + RS
WC = RB * 128
NP = (NC - 2) * NU
PC = 3 * WC // NP
WB = 4
HIGH_PIECES = {0: (0,), 1: (1, 2), 2: (3,), 3: (4,), 5: (5, 6), 7: (7,)}
LOW_PIECES = {1: (0,), 2: (1, 2), 3: (3,), 4: (4,), 6: (5,), 7: (6, 7)}
EPS = 1e-5
MASKED = -(2.0 ** 64)
PICKED = -3.0e38
ROUTED_SCALE = 2.5
QA = 1
RU = 4

CHAIN_FIRST, CHAIN_INNER = 7, 31


def wait(eng, sem, value):
    if isinstance(value, int) and value <= 0:
        return
    eng.wait_ge(sem, value)


def build(nc, x, ctx_in, mask, wq, wk, wv, wo, bq, bk, bv, bo, gate_w, gate_b,
          w_all, consts, sel, onehot, out):
    ctx = ExitStack()
    with ctx:
        def sb(name, shape, dt):
            return ctx.enter_context(nc.sbuf_tensor(name, shape, dt))

        def sem(name):
            return ctx.enter_context(nc.semaphore(name))

        x_v = x.rearrange("(c b) t d -> c t b d", b=CB)
        c_v = ctx_in.rearrange("(c b) t d -> c t b d", b=CB)
        m_v = mask.rearrange("(c b) t s -> c t b s", b=CB)
        out_v = out.rearrange("(c b) t d -> c t b d", b=CB)

        cst = sb("cst", [128, 128 + 4 + 4 + 64], F32)
        ident, qmask, amask, tri = cst[:, 0:128], cst[:, 128:132], cst[:, 132:136], cst[:, 136:200]
        ident_b = sb("ident_b", [128, 128], BF16)
        ident_h = sb("ident_h", [128, 128], F16)
        ones_b = sb("ones_b", [128, 128], BF16)
        row_sel = sb("row_sel", [128, HQ, T], BF16)
        wq_s, wk_s = sb("wq_s", [128, 128], F32), sb("wk_s", [128, 128], F32)
        wv_s, wo_s = sb("wv_s", [128, 128], F32), sb("wo_s", [128, 128], F32)
        gw_s = sb("gw_s", [128, NE], F32)
        bq_s, bk_s = sb("bq_s", [128, 1], F32), sb("bk_s", [128, 1], F32)
        bv_s, bo_s = sb("bv_s", [128, 128], F32), sb("bo_s", [128, 128], F32)
        gb_s = sb("gb_s", [128, NE], F32)
        onehot_s = sb("onehot_s", [128, RR * 128], F16)
        sel_s = sb("sel_s", [128, 4, 4, 128], F16)
        q_sel, k_sel = (sel_s[:, 0], sel_s[:, 1]), (sel_s[:, 2], sel_s[:, 3])

        w_hi, w_lo = sb("w_hi", [128, 3 * WC], F16), sb("w_lo", [128, 3 * WC], F16)
        x2 = sb("x2", [128, NC * CT], F32)
        x2t_hi = sb("x2t_hi", [128, NC * CT], F16)
        x2t_lo = sb("x2t_lo", [128, NC * CT], F16)
        rwt = sb("rwt", [128, NC * CT], F16)

        x_in, c_in = sb("x_in", [128, CB, D], F32), sb("c_in", [128, CB, D], F32)
        m_in = sb("m_in", [128, CB, T], I32)
        mbias = sb("mbias", [128, CB, T], BF16)
        w_in = sb("w_in", [128, WB, PC], F32)
        stats = sb("stats", [128, CB, 6], F32)
        mv, mv2 = sb("mv", [128, CB, 2], F32), sb("mv2", [128, CB, 2], F32)
        var, var2 = sb("var", [128, CB], F32), sb("var2", [128, CB], F32)
        rstd, rstd2 = sb("rstd", [128, CB], F32), sb("rstd2", [128, CB], F32)
        spare_p, spare_v = sb("spare_p", [128, 8], F32), sb("spare_v", [128, 16], F32)
        spare_a = sb("spare_a", [128, 1], F32)
        minus_half = sb("minus_half", [128, CB], F32)
        xn = sb("xn", [128, CB, D], F32)
        xnt, cnt = sb("xnt", [128, CT], F32), sb("cnt", [128, CT], F32)
        qf, kf = sb("qf", [128, CT], F32), sb("kf", [128, CT], F32)
        q_hi, q_lo = sb("q_hi", [128, CB, T], F16), sb("q_lo", [128, CB, T], F16)
        k_hi, k_lo = sb("k_hi", [128, CB, T], F16), sb("k_lo", [128, CB, T], F16)
        q_st = sb("q_st", [128, 2, HQ, 4, T], F16)
        q_all = sb("q_all", [128, 4 * T], F16)
        k_st = sb("k_st", [128, 2, 4, T], F16)
        v_st = sb("v_st", [128, CB, D], F32)
        v_s = sb("v_s", [128, CB, NH, 2, VW], F16)
        negmax = sb("negmax", [128, 128], BF16)
        max_rows = sb("max_rows", [128, T], BF16)
        p_s = sb("p_s", [128, 2, UH * T], F32)
        p_hi, p_lo = sb("p_hi", [128, 2, UH * T], F16), sb("p_lo", [128, 2, UH * T], F16)
        rsum = sb("rsum", [128, NH], F32)
        o_n = sb("o_n", [128, NH, DK], F32)
        o_t = sb("o_t", [128, CB, T], F32)
        xn2 = sb("xn2", [128, CB, D], F32)
        x2tf = sb("x2tf", [128, CT], F32)
        esig = sb("esig", [128, CB, NE], F32)
        score, choice = sb("score", [128, CB, NE], F32), sb("choice", [128, CB, NE], F32)
        top_a, top_b = sb("top_a", [128, CB * NG, 4], F32), sb("top_b", [128, CB * NG, 4], F32)
        top_c, top_d = sb("top_c", [128, CB * NG, 4], F32), sb("top_d", [128, CB * NG, 4], F32)
        gscore = sb("gscore", [128, CB, NG], F32)
        cmp_a, cmp_b = sb("cmp_a", [128, CB, NG * NG], F32), sb("cmp_b", [128, CB, NG * NG], F32)
        gkeep = sb("gkeep", [128, CB, NG], F32)
        best = sb("best", [128, CB, TK], F32)
        rest = sb("rest", [128, CB, NE], F32)
        wsum = sb("wsum", [128, CB], F32)
        rw = sb("rw", [128, CB, NE], F32)
        rwcat = sb("rwcat", [128, CB, 2, NE], F16)

        sg, gu = p_s[:, :, 0:CT], p_s[:, :, CT:2 * CT]
        q_flat = q_st[:, :, :, :, :].rearrange("p a h j t -> p (a h j t)")
        h_f = q_flat[:, 0:4 * CT].bitcast(F32).rearrange("p (k n) -> p k n", k=2)
        h_parts = q_flat[:, 4 * CT:8 * CT].rearrange("p (a k n) -> p a k n", a=2, k=2)
        h_hi, h_lo = h_parts[:, 0], h_parts[:, 1]
        y_s, o_st = xnt, xn

        ps = ctx.enter_context(nc.psum_tensor("ps", [128, 8 * 512], F32))

        def bank(n, k=1):
            return ps[:, 512 * n:512 * (n + k)]

        s_cst, s_proj = sem("shape_constants_loaded"), sem("projection_weights_loaded")
        s_const = sem("other_weights_loaded")
        s_prep = sem("constants_prepared")
        s_x, s_c, s_m = sem("x_loaded"), sem("ctx_loaded"), sem("mask_loaded")
        s_w = [sem(f"weights_loaded_{k}") for k in range(WB)]
        s_oh = sem("onehot_loaded")
        s_sel = sem("selectors_loaded")
        s_whi = sem("weights_high")
        s_wsplit = sem("weights_split")
        s_xb = sem("residual_base_made")
        s_mb = sem("mask_bias_made")
        s_vc = sem("chain_vector")
        s_pc = sem("chain_pool")
        s_var, s_rs = sem("x_variance"), sem("x_deviation")
        s_var2, s_rs2 = sem("x2_variance"), sem("x2_deviation")
        s_xn = sem("x_normalised")
        s_b6, s_b7 = sem("bank6_read"), sem("bank7_read_after_last_chunk")
        s_xt, s_ct, s_qp, s_kp = sem("x_transposed"), sem("ctx_transposed"), sem("q_projected"), sem("k_projected")
        s_vp = sem("v_projected")
        s_qh, s_kh = sem("q_high"), sem("k_high")
        s_ql, s_kl = sem("q_low"), sem("k_low")
        s_ks, s_qs = sem("k_stack_selected"), sem("q_stack_selected")
        s_kst = sem("k_stack_ready")
        s_qsa, s_qsv = sem("q_stacks_by_scalar"), sem("q_stacks_by_vector")
        s_v = sem("v_ready")
        s_sc, s_max = sem("scores_ready"), sem("max_taken")
        s_mxt, s_rows = sem("max_transposed"), sem("max_rows_ready")
        s_sts, s_st = sem("key_scores_summed"), sem("exponents_ready")
        s_ph, s_plv, s_plp = sem("probs_high"), sem("probs_low_by_vector"), sem("probs_low_by_pool")
        s_vb, s_vh = sem("v_biased"), sem("v_high")
        s_exp, s_pv = sem("probs_ready"), sem("pv_done")
        s_on, s_ot = sem("heads_normalised"), sem("heads_transposed")
        s_wo = sem("attention_out")
        s_xn2, s_x2t = sem("x2_normalised"), sem("x2_transposed")
        s_x2h, s_x2l = sem("x2t_high"), sem("x2t_low")
        s_gl = sem("gate_logits")
        s_rw, s_rwt = sem("routing_ready"), sem("routing_transposed")
        s_g, s_u = sem("gate_ready"), sem("up_ready")
        s_rwe = sem("routing_expanded")
        s_sg, s_gup = sem("silu_ready"), sem("gate_times_up")
        s_h, s_hh, s_hl = sem("hidden_ready"), sem("hidden_high"), sem("hidden_low")
        s_d = sem("down_done")
        s_yc, s_yt, s_fin, s_out = sem("y_copied"), sem("y_transposed"), sem("output_made"), sem("output_stored")

        block = ctx.enter_context(nc.Block())

        USES = {
            "head": ["ct", "xt", "k", "q", "v", "selq0", "selq1"],
            "first": ["selq2", "xt", "ct", "selq3", "q", "ot0", "selq0", "k", "ot1", "selq1", "ot2", "v"],
            "inner": ["selq2", "ot3", "wo", "xt", "ct", "selq3", "x2t", "gate", "q", "ot0",
                      "selq0", "k", "ot1", "selq1", "ot2", "v", "rwt"],
            "last": ["selq2", "ot3", "wo", "selq3", "x2t", "gate", "ot0", "ot1", "ot2", "rwt"],
        }

        def before(c, use):
            if isinstance(c, str):
                kind, count = "head", 0
            elif isinstance(c, int) and c == 0:
                kind, count = "first", len(USES["head"])
            else:
                kind = "last" if isinstance(c, int) else "inner"
                count = len(USES["head"]) + len(USES["first"]) + (c - 1) * len(USES["inner"])
            return count + USES[kind].index(use)

        MAIN, TAIL = (bank(6), s_b6), (bank(7), s_b7)
        TAIL_USES = ["ot3", "wo", "x2t", "gate", "rwt"]
        HEAD_BANK = {"ct": 2, "xt": 3, "k": 4, "q": 5, "v": 7, "selq0": 6, "selq1": 2}

        def head(use):
            return bank(HEAD_BANK[use]), s_b6

        def tail(use):
            return TAIL_USES.index(use)

        def after(c, use):
            return before(c, use) + 1

        @block.sync
        def _(sp):
            sp.dma_start(x_in[:, :, :], x_v[0]).then_inc(s_x, 16)
            sp.dma_start(c_in[:, :, :], c_v[0]).then_inc(s_c, 16)
            sp.dma_start(cst[:, :], consts).then_inc(s_cst, 16)
            for dst, src in ((wk_s[:, :], wk), (bk_s[:, :], bk), (wq_s[:, :], wq), (bq_s[:, :], bq), (wv_s[:, :], wv)):
                sp.dma_start(dst, src).then_inc(s_proj, 16)
            sp.dma_start(m_in[:, :, :], m_v[0]).then_inc(s_m, 16)
            for dst, src in ((bv_s[:, :], bv), (bo_s[:, :], bo), (gb_s[:, :], gate_b)):
                sp.dma_start(dst, src.partition_broadcast(128)).then_inc(s_const, 16)
            for dst, src in ((wo_s[:, :], wo), (gw_s[:, :], gate_w)):
                sp.dma_start(dst, src).then_inc(s_const, 16)
            sp.dma_start(sel_s[:, :, :, :], sel).then_inc(s_sel, 16)
            sp.dma_start(onehot_s[:, :], onehot).then_inc(s_oh, 16)
            for k in range(WB):
                sp.dma_start(w_in[:, k, :], w_all[:, k * PC:(k + 1) * PC]).then_inc(s_w[k], 16)

            def pieces(turn):
                for k in range(WB):
                    piece = turn * WB + k
                    sp.wait_ge(s_wsplit, piece - WB + 1)
                    sp.dma_start(w_in[:, k, :], w_all[:, bass.ds(piece * PC, PC)]).then_inc(s_w[k], 16)

            def load_mask(c):
                sp.wait_ge(s_mb, 2 * c)
                sp.dma_start(m_in[:, :, :], m_v[bass.ds(c, 1)].squeeze(0)).then_inc(s_m, 16)

            def load_x_and_ctx(c):
                sp.wait_ge(s_xn, c)
                sp.wait_ge(s_xb, c)
                sp.dma_start(x_in[:, :, :], x_v[bass.ds(c, 1)].squeeze(0)).then_inc(s_x, 16)
                sp.wait_ge(s_ct, c)
                sp.dma_start(c_in[:, :, :], c_v[bass.ds(c, 1)].squeeze(0)).then_inc(s_c, 16)

            load_x_and_ctx(1)
            load_mask(1)
            load_x_and_ctx(2)
            with sp.Fori(1, NC - 2) as c:
                load_mask(c + 1)
                pieces((c - 1) * (NU // WB) + 1)
                load_x_and_ctx(c + 2)
                pieces((c - 1) * (NU // WB) + 2)
            load_mask(NC - 1)
            pieces(NP // WB - 1)
            for c in range(NC):
                sp.wait_ge(s_fin, c + 1)
                sp.dma_start(out_v[c], o_st[:, :, :]).then_inc(s_out, 16)
                sp.wait_ge(s_out, 16 * (c + 1))

        @block.gpsimd
        def _(pool):
            g = nc.gpsimd

            spare = {}

            def carry_wait(place):
                k = spare.setdefault(place, len(spare))
                g.tensor_tensor(spare_p[:, k:k + 1], minus_half[:, 0:1], minus_half[:, 1:2], ALU.add)

            g.memset(ones_b[:, :], 1.0).then_inc(s_prep, 1)
            g.memset(negmax[:, :], 0.0).then_inc(s_prep, 1)
            g.memset(v_s[:, :, :, 0, :], 1.0).then_inc(s_prep, 1)
            g.memset(v_s[:, :, :, 1, :], 0.0).then_inc(s_prep, 1)
            g.memset(row_sel[:, :, :], 1.0).then_inc(s_pc, 1)
            g.memset(minus_half[:, :], -0.5).then_inc(s_pc, 1)
            pool.wait_ge(s_pc, 2)

            def deviation(c):
                pool.wait_ge(s_var, c + 1)
                wait(pool, s_xn, c)
                g.tensor_tensor(rstd[:, :], var[:, :], minus_half[:, :], ALU.pow).then_inc(s_rs, 1)

            deviation(0)
            pool.wait_ge(s_cst, 16)
            g.tensor_copy(ident_b[:, :], ident).then_inc(s_prep, 1)
            g.tensor_copy(ident_h[:, :], ident).then_inc(s_prep, 1)
            for h in range(HQ):
                g.tensor_scalar(row_sel[:, h, :], row_sel[:, h, :], amask[:, h:h + 1], None, ALU.mult).then_inc(s_prep, 1)

            def prepare(c, lo, hi):
                carry_wait(("mask", lo))
                g.tensor_scalar(mbias[:, lo:hi, :], m_in[:, lo:hi, :], 0.0, MASKED,
                                ALU.is_equal, ALU.mult).then_inc(s_mb, 1)

            def base(c):
                bo_b = bo_s[:, :].unsqueeze(1).to_broadcast([128, CB, D])
                g.tensor_tensor(x2[:, bass.ds(c * CT, CT)].rearrange("p (b d) -> p b d", b=CB), x_in[:, :, :], bo_b,
                                ALU.add).then_inc(s_xb, 1)

            def v_bias(c, staged):
                wait(pool, s_b6, staged)
                g.tensor_tensor(v_st[:, :, :], v_st[:, :, :], bv_s[:, :].unsqueeze(1).to_broadcast([128, CB, D]),
                                ALU.add).then_inc(s_vb, 1)

            def v_low(c):
                wait(pool, s_vb, c + 1)
                wait(pool, s_vh, c + 1)
                g.tensor_tensor(v_s[:, :, :, 1, 0:DK], v_st[:, :, :].rearrange("p b (h e) -> p b h e", h=NH),
                                v_s[:, :, :, 0, 0:DK], ALU.subtract).then_inc(s_v, 1)

            def probs_low(c, u):
                n = NU * c + u
                wait(pool, s_ph, n + 1)
                wait(pool, s_pv, n - 1)
                half = slice(CT, 2 * CT)
                g.tensor_tensor(p_lo[:, u % 2, half], p_s[:, u % 2, half], p_hi[:, u % 2, half],
                                ALU.subtract).then_inc(s_plp, 1)

            def low_part(c, low, high, full, ready, signal, picked):
                wait(pool, ready, c + 1)
                wait(pool, picked, CB * c)
                g.tensor_tensor(low[:, :, :].rearrange("p b t -> p (b t)"), full[:, :],
                                high[:, :, :].rearrange("p b t -> p (b t)"), ALU.subtract).then_inc(signal, 1)

            def low_k(c):
                low_part(c, k_lo, k_hi, kf, s_kh, s_kl, s_ks)

            def low_q(c):
                low_part(c, q_lo, q_hi, qf, s_qh, s_ql, s_qs)

            def x2t_low(c):
                wait(pool, s_x2h, c + 1)
                g.tensor_tensor(x2t_lo[:, bass.ds(c * CT, CT)], x2tf[:, :], x2t_hi[:, bass.ds(c * CT, CT)],
                                ALU.subtract).then_inc(s_x2l, 1)

            def deviation2(c):
                pool.wait_ge(s_var2, c + 1)
                wait(pool, s_xn2, c)
                g.tensor_tensor(rstd2[:, :], var2[:, :], minus_half[:, :], ALU.pow).then_inc(s_rs2, 1)

            pool.wait_ge(s_m, 16)
            prepare(0, 0, 2)
            prepare(0, 2, CB)
            low_k(0)
            low_q(0)
            pool.wait_ge(s_const, 16 * 5)
            base(0)
            v_bias(0, after("head", "v"))
            v_low(0)

            def low_weights(c, u):
                piece = NU * (c - 1) + u
                pool.wait_ge(s_whi, piece + 1)
                at = bass.ds(piece * PC, PC)
                g.tensor_tensor(w_lo[:, at], w_in[:, u % WB, :], w_hi[:, at], ALU.subtract).then_inc(s_wsplit, 1)

            def chunk(c, prev, nxt):
                for u in range(NU):
                    if u == 0 and nxt:
                        deviation(c + 1)
                    if u == 4 and nxt:
                        low_q(c + 1)
                    if u == 6 and nxt:
                        low_k(c + 1)
                    if u == 0 and prev:
                        v_low(c)
                    if u == 2 and prev:
                        deviation2(c - 1)
                    probs_low(c, u)
                    if u == 0 and nxt:
                        base(c + 1)
                    if u == 4 and prev:
                        x2t_low(c - 1)
                    if u == 7 and nxt:
                        v_bias(c + 1, after(c, "v"))
                    if prev and nxt:
                        for piece in LOW_PIECES.get(u, ()):
                            low_weights(c, piece)
                    if u == 3 and nxt:
                        pool.wait_ge(s_m, 16 * (c + 2))
                        pool.wait_ge(s_st, NU * c + 4)
                        prepare(c + 1, 0, 2)
                    if u == 0 and prev:
                        pool.wait_ge(s_st, NU * c)
                        prepare(c, 2, CB)

            chunk(0, False, True)
            with pool.Fori(1, NC - 1) as c:
                chunk(c, True, True)
            chunk(NC - 1, True, False)

            def low(n, k):
                pool.wait_ge(s_h, n + 1)
                pool.wait_ge(s_hh, n + 1)
                wait(pool, s_d, n - 1)
                g.tensor_tensor(h_lo[:, k % 2, :], h_f[:, k % 2, :], h_hi[:, k % 2, :], ALU.subtract).then_inc(s_hl, 1)

            low(0, 0)
            low(1, 1)
            deviation2(NC - 1)
            for k in range(RU):
                low(RS + k, k)
                if k == 1:
                    x2t_low(NC - 1)
            with pool.Fori(1, RR // RU) as turn:
                r = turn * RU
                for k in range(RU):
                    low(r + (RS + k), k)

            with pool.Fori(1, NC) as c:
                low(c * RB, 0)
                low(c * RB + 1, 1)
                with pool.Fori(0, RR // RU) as turn:
                    r = turn * RU
                    for k in range(RU):
                        low(c * RB + r + (RS + k), k)

        @block.scalar
        def _(act):
            a = nc.scalar

            def copy_xnt(c, place=MAIN):
                wait(act, s_xt, c + 1)
                wait(act, s_qp, c)
                a.activation(xnt[:, :], place[0], ACT.Copy).then_inc(place[1], 1)

            def copy_cnt(c, place=MAIN):
                wait(act, s_ct, c + 1)
                wait(act, s_kp, c)
                wait(act, s_vp, c)
                a.activation(cnt[:, :], place[0], ACT.Copy).then_inc(place[1], 1)

            def copy_q(c, place=MAIN):
                wait(act, s_qp, c + 1)
                wait(act, s_ql, c)
                a.activation(qf[:, :], place[0], ACT.Identity, bias=bq_s[:, 0:1]).then_inc(place[1], 1)

            def copy_k(c, place=MAIN):
                wait(act, s_kp, c + 1)
                wait(act, s_kl, c)
                a.activation(kf[:, :], place[0], ACT.Identity, bias=bk_s[:, 0:1]).then_inc(place[1], 1)

            def high_q(c, done):
                act.wait_ge(s_b6, done)
                wait(act, s_qs, CB * c)
                a.activation(q_hi[:, :, :].rearrange("p b t -> p (b t)"), qf[:, :], ACT.Copy).then_inc(s_qh, 1)

            def high_k(c, done):
                act.wait_ge(s_b6, done)
                wait(act, s_ks, CB * c)
                a.activation(k_hi[:, :, :].rearrange("p b t -> p (b t)"), kf[:, :], ACT.Copy).then_inc(s_kh, 1)

            def stack_k(c, b):
                n = CB * c + b
                wait(act, s_ks, n + 1)
                wait(act, s_sts, 2 * n - 2)
                a.activation(k_st[:, b % 2, :, :].rearrange("p j t -> p (j t)"), bank(0), ACT.Copy).then_inc(s_kst, 1)

            def stack_q(c, b, place=MAIN):
                n = CB * c + b
                wait(act, s_qs, n + 1)
                wait(act, s_qsa, n)
                wait(act, s_qsv, n)
                a.activation(q_all[:, :], place[0], ACT.Copy).then_inc(place[1], 1)

            def separate_q(c, b, done):
                n = CB * c + b
                wait(act, s_sts, 2 * n - 2)
                wait(act, s_b6, done)
                for h in range(QA):
                    ins = a.activation(q_st[:, b % 2, h, :, :].rearrange("p j t -> p (j t)"), q_all[:, :], ACT.Copy,
                                       scale=qmask[:, h:h + 1])
                ins.then_inc(s_qsa, 1)

            def high_weights(c, u):
                piece = NU * (c - 1) + u
                act.wait_ge(s_w[u % WB], 16 * ((c - 1) * (NU // WB) + (u // WB + 1)))
                a.activation(w_hi[:, bass.ds(piece * PC, PC)], w_in[:, u % WB, :], ACT.Copy).then_inc(s_whi, 1)

            def high_v(c):
                act.wait_ge(s_vb, c + 1)
                wait(act, s_pv, NU * c)
                a.activation(v_s[:, :, :, 0, 0:DK], v_st[:, :, :].rearrange("p b (h e) -> p b h e", h=NH),
                             ACT.Copy).then_inc(s_vh, 1)

            def exp(c, u):
                n = NU * c + u
                wait(act, s_st, n + 1)
                wait(act, s_plv, n - 1)
                wait(act, s_plp, n - 1)
                a.activation(p_s[:, u % 2, :], bank(2 + 2 * (u % 2), 2), ACT.Exp, scale=DK ** -0.5).then_inc(s_exp, 1)

            def high_probs(c, u):
                n = NU * c + u
                act.wait_ge(s_exp, n + 1)
                wait(act, s_pv, n - 1)
                a.activation(p_hi[:, u % 2, :], p_s[:, u % 2, :], ACT.Copy).then_inc(s_ph, 1)

            def copy_ot(c, b, place=MAIN):
                wait(act, s_ot, CB * c + b + 1)
                wait(act, s_wo, c)
                a.activation(o_t[:, b, :], place[0][:, 0:T], ACT.Copy).then_inc(place[1], 1)

            def copy_x2t(c, place=MAIN):
                wait(act, s_x2t, c + 1)
                wait(act, s_gl, c)
                wait(act, s_x2l, c)
                a.activation(x2tf[:, :], place[0], ACT.Copy).then_inc(place[1], 1)

            def high_x2t(c, done, place=MAIN):
                act.wait_ge(place[1], done)
                a.activation(x2t_hi[:, bass.ds(c * CT, CT)], x2tf[:, :], ACT.Copy).then_inc(s_x2h, 1)

            def copy_v(c, place=MAIN):
                wait(act, s_vp, c + 1)
                wait(act, s_v, c)
                a.activation(v_st[:, :, :].rearrange("p b d -> p (b d)"), place[0], ACT.Copy).then_inc(place[1], 1)

            def exp_gate(c, place=MAIN):
                wait(act, s_gl, c + 1)
                wait(act, s_rw, c)
                a.activation(esig[:, :, :].rearrange("p b e -> p (b e)"), place[0][:, 0:CB * NE], ACT.Exp,
                             scale=-1.0).then_inc(place[1], 1)

            def copy_rwt(c, place=MAIN):
                wait(act, s_rwt, c + 1)
                src = place[0][:, 0:CT // 2].bitcast(F16)
                a.activation(rwt[:, bass.ds(c * CT, CT)], src, ACT.Copy).then_inc(place[1], 1)

            act.wait_ge(s_prep, 1)
            a.activation(spare_a[:, :], ones_b[:, 0:1], ACT.Exp)
            act.wait_ge(s_cst, 16)
            act.wait_ge(s_proj, 16 * 5)
            copy_cnt(0, head("ct"))
            copy_xnt(0, head("xt"))
            copy_k(0, head("k"))
            high_k(0, after("head", "k"))
            copy_q(0, head("q"))
            high_q(0, after("head", "q"))
            copy_v(0, head("v"))
            act.wait_ge(s_prep, 3)
            high_v(0)
            stack_k(0, 0)
            stack_q(0, 0, head("selq0"))
            separate_q(0, 0, after("head", "selq0"))
            stack_q(0, 1, head("selq1"))
            separate_q(0, 1, after("head", "selq1"))

            def chunk(c, prev, nxt):
                for u in range(NU):
                    b = u // 2
                    if u == 1 and prev:
                        copy_ot(c - 1, CB - 1)
                    if u == 2 and nxt:
                        copy_xnt(c + 1)
                    if u == 3 and prev:
                        copy_x2t(c - 1)
                    if u in (4, 6, 7):
                        copy_ot(c, u // 2 - 2 + u % 2)

                    exp(c, u)
                    if u == 0 and prev:
                        high_v(c)
                    if u == 2 and nxt:
                        copy_cnt(c + 1)
                    if u == 3 and prev:
                        exp_gate(c - 1)
                    if u == 5 and nxt:
                        stack_q(c + 1, 0)
                    if u == 7 and nxt:
                        copy_v(c + 1)
                    if u == 4:
                        separate_q(c, 3, after(c, "selq3"))
                    elif u == 6 and nxt:
                        separate_q(c + 1, 0, after(c, "selq0"))
                    if u in (0, 2, 4):
                        stack_k(c, b + 1)
                    elif u == 6 and nxt:
                        stack_k(c + 1, 0)
                    high_probs(c, u)
                    if u == 3 and nxt:
                        copy_q(c + 1)
                        high_q(c + 1, after(c, "q"))
                    if u == 5 and nxt:
                        copy_k(c + 1)
                        high_k(c + 1, after(c, "k"))
                    if u == 1:
                        separate_q(c, 2, after(c, "selq2"))
                    elif u == 7 and nxt:
                        separate_q(c + 1, 1, after(c, "selq1"))
                    if u in (0, 2):
                        stack_q(c, b + 2)
                    elif u == 6 and nxt:
                        stack_q(c + 1, 1)
                    if u == 4 and prev:
                        high_x2t(c - 1, after(c, "x2t"))
                    if prev and nxt:
                        for piece in HIGH_PIECES.get(u, ()):
                            high_weights(c, piece)
                    if u == 7 and prev:
                        copy_rwt(c - 1)

            chunk(0, False, True)
            with act.Fori(1, NC - 1) as c:
                chunk(c, True, True)
            chunk(NC - 1, True, False)

            def silu(n, k):
                act.wait_ge(s_g, n + 1)
                wait(act, s_gup, n - 1)
                a.activation(sg[:, k % 2, :], bank(k % 2), ACT.Silu).then_inc(s_sg, 1)

            def high(n, k):
                act.wait_ge(s_h, n + 1)
                wait(act, s_d, n - 1)
                a.activation(h_hi[:, k % 2, :], h_f[:, k % 2, :], ACT.Copy).then_inc(s_hh, 1)

            def y_copy(c):
                wait(act, s_d, RB * (c + 1))
                wait(act, s_yt, c)
                a.activation(y_s[:, :], bank(6), ACT.Copy).then_inc(s_yc, 1)

            def turn_of_blocks(first):
                for k in range(RU):
                    silu(first + k, k)
                    high(first + (k - 1), k + 1)

            silu(0, 0)
            copy_ot(NC - 1, CB - 1, TAIL)
            silu(1, 1)
            high(0, 0)
            for k in range(2 * RU):
                silu(RS + k, k)
                if k == 4:
                    exp_gate(NC - 1, TAIL)
                high(RS + k - 1, k + 1)
                if k == 2:
                    copy_x2t(NC - 1, TAIL)
                    high_x2t(NC - 1, tail("x2t") + 1, TAIL)
            with act.Fori(2, RR // RU) as turn:
                turn_of_blocks(turn * RU + RS)
            copy_rwt(NC - 1, TAIL)

            with act.Fori(1, NC) as c:
                n = c * RB
                silu(n, 0)
                high(n - 1, 1)
                silu(n + 1, 1)
                high(n, 0)
                y_copy(c - 1)
                with act.Fori(0, RR // RU) as turn:
                    turn_of_blocks(n + turn * RU + RS)
            high(NC * RB - 1, 1)
            y_copy(NC - 1)

        @block.vector
        def _(dve):
            v = nc.vector

            spare = {}

            def carry_wait(place):
                k = spare.setdefault(place, len(spare))
                v.memset(spare_v[:, k:k + 1], 0.0)

            state = {"base": 0, "k": 0}

            def link(ins):
                ins.then_inc(s_vc, 1)
                state["k"] += 1
                dve.wait_ge(s_vc, state["base"] + state["k"])

            def moments(src, mv_, var_, signal):
                carry_wait(("stats", mv_ is mv))
                for b in range(CB):
                    ins = v.bn_stats(stats[:, b, :], src(b))
                link(ins)
                carry_wait(("aggregate", mv_ is mv))
                for b in range(CB):
                    ins = v.bn_aggr(mv_[:, b, :], stats[:, b, :])
                link(ins)
                v.tensor_scalar(var_[:, :], mv_[:, :, 1], EPS, None, ALU.add).then_inc(signal, 1)

            def normalise(dst, src, mv_, rstd_, signal):
                for b in range(CB):
                    ins = v.tensor_scalar(dst[:, b, :], src(b), mv_[:, b, 0:1], rstd_[:, b:b + 1],
                                          ALU.subtract, ALU.mult)
                ins.then_inc(signal, 1)

            def x_moments(c):
                wait(dve, s_x, 16 * (c + 1))
                wait(dve, s_rs, c)
                moments(lambda b: x_in[:, b, :], mv, var, s_var)

            def norm_x(c):
                wait(dve, s_rs, c + 1)
                wait(dve, s_xt, c)
                normalise(xn, lambda b: x_in[:, b, :], mv, rstd, s_xn)

            def separate_q(c, b, done):
                n = CB * c + b
                wait(dve, s_sts, 2 * n - 2)
                wait(dve, s_b6, done)
                for h in range(QA, HQ):
                    ins = v.tensor_scalar(q_st[:, b % 2, h, :, :].rearrange("p j t -> p (j t)"), q_all[:, :],
                                          qmask[:, h:h + 1], None, ALU.mult)
                ins.then_inc(s_qsv, 1)

            def row_max(c, u):
                n = NU * c + u
                half = u % 2
                wait(dve, s_sc, n + 1)
                wait(dve, s_mxt, n - 1)
                dst = negmax[:, 64 * half:64 * half + 64].rearrange("p (j q) -> p j q", j=2)[:, :, 0:HQ]
                v.tensor_reduce(dst, bank(0, 2).rearrange("p (j h s) -> p j h s", j=2, h=HQ), AX.X, ALU.max,
                                negate=True).then_inc(s_max, 1)

            def copy_rows(c, u):
                n = NU * c + u
                p0 = 64 * (u % 2)
                wait(dve, s_mxt, n + 1)
                wait(dve, s_st, n - 1)
                v.tensor_copy(max_rows[p0:p0 + 64, :], bank(7)[p0:p0 + 64, 0:T]).then_inc(s_rows, 1)

            def probs_low(c, u):
                n = NU * c + u
                wait(dve, s_ph, n + 1)
                wait(dve, s_pv, n - 1)
                v.tensor_tensor(p_lo[:, u % 2, 0:CT], p_s[:, u % 2, 0:CT], p_hi[:, u % 2, 0:CT],
                                ALU.subtract).then_inc(s_plv, 1)

            def norm_heads(c, b):
                wait(dve, s_pv, NU * c + 2 * b + 2)
                wait(dve, s_ot, CB * c + b)
                o = bank(7)[:, 256:256 + NH * VW].rearrange("p (h e) -> p h e", e=VW)
                link(v.reciprocal(rsum[:, :], o[:, :, DK]))
                v.tensor_tensor(o_n[:, :, :], o[:, :, 0:DK], rsum[:, :].unsqueeze(2).to_broadcast([128, NH, DK]),
                                ALU.mult).then_inc(s_on, 1)

            def x2_chunk(c):
                return x2[:, bass.ds(c * CT, CT)]

            def residual(c, place=MAIN):
                wait(dve, s_wo, c + 1)
                v.tensor_tensor(x2_chunk(c), x2_chunk(c), place[0], ALU.add).then_inc(place[1], 1)

            def x2_moments(c, done, place=MAIN):
                dve.wait_ge(place[1], done)
                wait(dve, s_rs2, c)
                moments(lambda b: x2[:, bass.ds(c * CT + b * D, D)], mv2, var2, s_var2)

            def norm_x2(c):
                wait(dve, s_rs2, c + 1)
                wait(dve, s_x2t, c)
                normalise(xn2, lambda b: x2[:, bass.ds(c * CT + b * D, D)], mv2, rstd2, s_xn2)

            flat = "p b e -> p (b e)"
            quad = "p b (i j) -> p b i j"

            def expert_scores(c, done, place=MAIN):
                dve.wait_ge(place[1], done)
                wait(dve, s_rwt, c)
                link(v.tensor_scalar(esig[:, :, :], esig[:, :, :], 1.0, None, ALU.add))
                link(v.reciprocal(score[:, :, :].rearrange(flat), esig[:, :, :].rearrange(flat)))
                link(v.tensor_tensor(choice[:, :, :], score[:, :, :],
                                     gb_s[:, :].unsqueeze(1).to_broadcast([128, CB, NE]), ALU.add))

            def group_scores():
                m = choice[:, :, :].rearrange(flat).rearrange("p (g e) -> p g e", e=GE)
                v.tensor_tensor(top_a[:, :, :], m[:, :, 0:4], m[:, :, 4:8], ALU.max)
                link(v.tensor_tensor(top_b[:, :, :], m[:, :, 0:4], m[:, :, 4:8], ALU.min))
                a_, b_, c_, d_ = top_a, top_b, top_c, top_d
                for w in (2, 1):
                    v.tensor_tensor(c_[:, :, 0:w], a_[:, :, 0:w], a_[:, :, w:2 * w], ALU.max)
                    v.tensor_tensor(d_[:, :, 0:w], a_[:, :, 0:w], a_[:, :, w:2 * w], ALU.min)
                    link(v.tensor_tensor(d_[:, :, 2:2 + w], b_[:, :, 0:w], b_[:, :, w:2 * w], ALU.max))
                    link(v.tensor_tensor(d_[:, :, 0:w], d_[:, :, 0:w], d_[:, :, 2:2 + w], ALU.max))
                    a_, b_, c_, d_ = c_, d_, a_, b_
                link(v.tensor_tensor(gscore[:, :, :].rearrange("p b g -> p (b g)"), a_[:, :, 0], b_[:, :, 0], ALU.add))

            def compare_groups():
                other = gscore[:, :, :].unsqueeze(2).to_broadcast([128, CB, NG, NG])
                own = gscore[:, :, :].unsqueeze(3).to_broadcast([128, CB, NG, NG])
                v.tensor_tensor(cmp_a[:, :, :].rearrange(quad, i=NG), other, own, ALU.is_gt)
                link(v.tensor_tensor(cmp_b[:, :, :].rearrange(quad, i=NG), other, own, ALU.is_ge))
                link(v.tensor_tensor(cmp_b[:, :, :], cmp_b[:, :, :], tri.unsqueeze(1).to_broadcast([128, CB, NG * NG]),
                                     ALU.mult))
                link(v.tensor_tensor(cmp_a[:, :, :], cmp_a[:, :, :], cmp_b[:, :, :], ALU.max))

            def keep_groups():
                link(v.tensor_reduce(gkeep[:, :, :], cmp_a[:, :, :].rearrange(quad, i=NG), AX.X, ALU.add))
                link(v.tensor_scalar(gkeep[:, :, :], gkeep[:, :, :], float(GK), None, ALU.is_lt))
                link(v.tensor_tensor(choice[:, :, :].rearrange("p b (g e) -> p b g e", e=GE),
                                     choice[:, :, :].rearrange("p b (g e) -> p b g e", e=GE),
                                     gkeep[:, :, :].unsqueeze(3).to_broadcast([128, CB, NG, GE]), ALU.mult))

            def find_best():
                carry_wait("best")
                for b in range(CB):
                    ins = v.max(best[:, b, :], choice[:, b, :])
                link(ins)

            def pick_experts():
                carry_wait("rest")
                for b in range(CB):
                    ins = v.match_replace(rest[:, b, :], best[:, b, :], choice[:, b, :], PICKED)
                link(ins)

            def sum_weights():
                link(v.scalar_tensor_tensor(rw[:, :, :].rearrange(flat), rest[:, :, :].rearrange(flat), PICKED,
                                            score[:, :, :].rearrange(flat), ALU.is_equal, ALU.mult))
                link(v.tensor_reduce(wsum[:, :], rw[:, :, :], AX.X, ALU.add))

            def weigh_experts():
                link(v.tensor_scalar(wsum[:, :], wsum[:, :], 1e-20, None, ALU.add))
                link(v.reciprocal(wsum[:, :], wsum[:, :]))
                link(v.scalar_tensor_tensor(rw[:, :, :], rw[:, :, :], ROUTED_SCALE,
                                            wsum[:, :].unsqueeze(2).to_broadcast([128, CB, NE]), ALU.mult, ALU.mult))
                link(v.tensor_copy(rwcat[:, :, 0, :], rw[:, :, :]))
                v.tensor_tensor(rwcat[:, :, 1, :], rw[:, :, :], rwcat[:, :, 0, :], ALU.subtract).then_inc(s_rw, 1)

            x_moments(0)
            norm_x(0)
            dve.wait_ge(s_const, 16 * 5)
            dve.wait_ge(s_prep, 10)
            separate_q(0, 0, after("head", "selq0"))
            separate_q(0, 1, after("head", "selq1"))
            row_max(0, 0)

            def chunk(c, prev, nxt):
                for u in range(NU):
                    copy_rows(c, u)
                    if u:
                        probs_low(c, u - 1)
                    elif prev:
                        probs_low(c - 1, NU - 1)
                    if u + 1 < NU:
                        row_max(c, u + 1)
                    elif nxt:
                        row_max(c + 1, 0)
                    if u == 0 and prev:
                        norm_heads(c - 1, CB - 1)
                    if u in (2, 4, 6):
                        norm_heads(c, u // 2 - 1)
                    if u == 0 and nxt:
                        x_moments(c + 1)
                    if u == 1 and prev:
                        residual(c - 1)
                    if u == 1 and nxt:
                        norm_x(c + 1)
                    if u == 1 and prev:
                        x2_moments(c - 1, after(c, "wo"))
                    if u in (2, 3):
                        separate_q(c, u, after(c, f"selq{u}"))
                    elif u == 6 and nxt:
                        separate_q(c + 1, 0, after(c, "selq0"))
                    if u == 2 and prev:
                        norm_x2(c - 1)
                    if u == 3 and prev:
                        expert_scores(c - 1, after(c, "gate"))
                    if u == 4 and prev:
                        group_scores()
                    if u == 5 and prev:
                        compare_groups()
                        keep_groups()
                    if u == 6 and prev:
                        find_best()
                        pick_experts()
                        sum_weights()
                    if u == 7 and prev:
                        weigh_experts()
                    if u == 7 and nxt:
                        separate_q(c + 1, 1, after(c, "selq1"))

            chunk(0, False, True)
            assert state["k"] == CHAIN_FIRST, state["k"]
            state["k"] = 0
            with dve.Fori(1, NC - 1) as c:
                state["base"] = CHAIN_FIRST + (c - 1) * CHAIN_INNER
                chunk(c, True, True)
            assert state["k"] == CHAIN_INNER, state["k"]
            state.update(base=CHAIN_FIRST + (NC - 2) * CHAIN_INNER, k=0)
            chunk(NC - 1, True, False)
            probs_low(NC - 1, NU - 1)
            norm_heads(NC - 1, CB - 1)

            def gate_up(n, k):
                dve.wait_ge(s_sg, n + 1)
                dve.wait_ge(s_u, n + 1)
                v.tensor_tensor(gu[:, k % 2, :], sg[:, k % 2, :], bank(2 + k % 2), ALU.mult).then_inc(s_gup, 1)

            def hidden(n, k, routed):
                wait(dve, s_gup, n + 1)
                wait(dve, s_hl, n - 1)
                if routed is None:
                    v.tensor_copy(h_f[:, k % 2, :], gu[:, k % 2, :]).then_inc(s_h, 1)
                else:
                    dve.wait_ge(s_rwe, routed + 1)
                    v.tensor_tensor(h_f[:, k % 2, :], gu[:, k % 2, :], bank(4 + k % 2), ALU.mult).then_inc(s_h, 1)

            def output(c):
                wait(dve, s_yt, c + 1)
                wait(dve, s_out, 16 * c)
                v.tensor_tensor(o_st[:, :, :].rearrange("p b d -> p (b d)"), x2_chunk(c), bank(7),
                                ALU.add).then_inc(s_fin, 1)

            def block(c, r, k):
                gate_up(c * RB + r + (RS + k), k)
                hidden(c * RB + r + (RS + k), k, c * RR + r + k)

            def shared_blocks(c):
                for k in range(RS):
                    gate_up(c * RB + k, k)
                    hidden(c * RB + k, k, None)

            shared_blocks(0)
            residual(NC - 1, TAIL)
            x2_moments(NC - 1, tail("wo") + 1, TAIL)
            block(0, 0, 0)
            norm_x2(NC - 1)
            TURNS = 6
            for r in range(1, TURNS * RU):
                block(0, r, 0) if r % 2 == 0 else block(0, r - 1, 1)
                if r == 6:
                    expert_scores(NC - 1, tail("gate") + 1, TAIL)
                if r == 9:
                    group_scores()
                if r == 12:
                    compare_groups()
                if r == 14:
                    keep_groups()
                if r == 16:
                    find_best()
                    pick_experts()
                if r == 19:
                    sum_weights()
                    weigh_experts()
            with dve.Fori(TURNS, RR // RU) as turn:
                for k in range(RU):
                    block(0, turn * RU, k)

            with dve.Fori(1, NC) as c:
                shared_blocks(c)
                with dve.Fori(0, RR // RU) as turn:
                    for k in range(RU):
                        block(c, turn * RU, k)
                output(c - 1)
            output(NC - 1)

        @block.tensor
        def _(pe):
            t = nc.tensor

            def heads4(ap):
                return ap.rearrange("p (h t) -> p h t", h=HQ)

            def transpose4(src, done, signal, place=MAIN):
                wait(pe, place[1], done)
                for b in range(CB):
                    ins = t.transpose(place[0][:, b * 128:(b + 1) * 128], src(b), ident)
                ins.then_inc(signal, 1)

            def x_transpose(c, done, place=MAIN):
                wait(pe, s_xn, c + 1)
                transpose4(lambda b: xn[:, b, :], done, s_xt, place)

            def ctx_transpose(c, done, place=MAIN):
                wait(pe, s_c, 16 * (c + 1))
                transpose4(lambda b: c_in[:, b, :], done, s_ct, place)

            def project(w, src, done, signal, place=MAIN):
                wait(pe, place[1], done)
                t.matmul(place[0], w[:, :], src[:, :], start=True, stop=True).then_inc(signal, 1)

            def project_v(done, place=MAIN):
                wait(pe, place[1], done)
                for b in range(CB):
                    ins = t.matmul(place[0][:, b * 128:(b + 1) * 128], cnt[:, b * 128:(b + 1) * 128], wv_s[:, :],
                                   start=True, stop=True)
                ins.then_inc(s_vp, 1)

            def pair(u):
                return [(jj, 2 * (u % 2) + jj) for jj in range(2)]

            def select(out, b, parts, selectors, signal):
                for j in range(4):
                    t.matmul(out[:, j * T:(j + 1) * T], selectors[0][:, j, :], parts[0][:, b, :],
                             start=True, stop=False)
                    ins = t.matmul(out[:, j * T:(j + 1) * T], selectors[1][:, j, :], parts[1][:, b, :],
                                   start=False, stop=True)
                ins.then_inc(signal, 1)

            def select_k(c, b, maxima):
                wait(pe, s_kl, c + 1)
                wait(pe, s_max, maxima)
                select(bank(0), b, (k_hi, k_lo), k_sel, s_ks)

            def select_q(c, b, done, place=MAIN):
                wait(pe, s_ql, c + 1)
                wait(pe, place[1], done)
                select(place[0], b, (q_hi, q_lo), q_sel, s_qs)

            def scores(c, u):
                n, b = NU * c + u, u // 2
                wait(pe, s_max, n)
                if u % 2 == 0:
                    wait(pe, s_kst, CB * c + b + 1)
                    wait(pe, s_qsa, CB * c + b + 1)
                    wait(pe, s_qsv, CB * c + b + 1)
                for jj, j in pair(u):
                    for h in range(HQ):
                        t.matmul(bank(jj)[:, h * T:(h + 1) * T], q_st[:, b % 2, h, j, :], k_st[:, b % 2, j, :],
                                 start=True, stop=False, skip_group_check=True)
                wait(pe, s_mb, 2 * c + (1 if b < 2 else 2))
                for jj, j in pair(u):
                    ins = t.matmul(heads4(bank(jj)), ident_b[:, :],
                                   mbias[:, b, :].unsqueeze(1).to_broadcast([128, HQ, T]), start=False, stop=True,
                                   skip_group_check=True)
                ins.then_inc(s_sc, 1)

            def key_scores(c, u):
                n, b, first = NU * c + u, u // 2, 2 + 2 * (u % 2)
                wait(pe, s_exp, n - 1)
                for jj, j in pair(u):
                    ins = t.matmul(heads4(bank(first + jj)), k_st[:, b % 2, j, :], q_st[:, b % 2, :, j, :],
                                   start=True, stop=False)
                ins.then_inc(s_sts, 1)

            def max_transpose(c, u):
                p0 = 64 * (u % 2)
                wait(pe, s_max, NU * c + u + 1)
                if u % 2:
                    wait(pe, s_on, CB * c + (u - 1) // 2)
                t.matmul(bank(7)[p0:p0 + 64, 0:T], negmax[:, p0:p0 + 64], ident_b[:, :],
                         start=True, stop=True).then_inc(s_mxt, 1)

            def mask_and_max(c, u):
                n, b, first = NU * c + u, u // 2, 2 + 2 * (u % 2)
                for jj, j in pair(u):
                    t.matmul(heads4(bank(first + jj)), mbias[:, b, :],
                             ident_b[:, :].unsqueeze(1).to_broadcast([128, HQ, T]), start=False, stop=True)
                wait(pe, s_rows, n + 1)
                for jj, j in pair(u):
                    q = slice(32 * j, 32 * j + 32)
                    for h in range(HQ):
                        ins = t.matmul(bank(first + jj)[:, h * T:(h + 1) * T], row_sel[q, h, :], max_rows[q, :],
                                       start=False, stop=True, skip_group_check=True)
                ins.then_inc(s_st, 1)

            def attend(c, u):
                n, b = NU * c + u, u // 2
                wait(pe, s_plv, n + 1)
                wait(pe, s_plp, n + 1)
                if u == 0:
                    wait(pe, s_v, c + 1)
                for hh in range(UH):
                    h = UH * (u % 2) + hh
                    o = bank(7)[:, 256 + h * VW:256 + (h + 1) * VW]
                    high, low = (p[:, u % 2, hh * T:(hh + 1) * T] for p in (p_hi, p_lo))
                    t.matmul(o, high, v_s[:, b, h, 0, :], start=True, stop=False)
                    t.matmul(o, high, v_s[:, b, h, 1, :], start=False, stop=False)
                    ins = t.matmul(o, low, v_s[:, b, h, 0, :], start=False, stop=True)
                ins.then_inc(s_pv, 1)

            def out_transpose(c, b, done, place=MAIN):
                wait(pe, s_on, CB * c + b + 1)
                wait(pe, place[1], done)
                t.transpose(place[0][:, 0:128], o_n[:, :, :].rearrange("p h e -> p (h e)"), ident).then_inc(s_ot, 1)

            def attention_out(done, place=MAIN):
                wait(pe, place[1], done)
                for b in range(CB):
                    ins = t.matmul(place[0][:, b * 128:(b + 1) * 128], o_t[:, b, :], wo_s[:, :], start=True, stop=True)
                ins.then_inc(s_wo, 1)

            def x2_transpose(c, done, place=MAIN):
                wait(pe, s_xn2, c + 1)
                transpose4(lambda b: xn2[:, b, :], done, s_x2t, place)

            def gate(done, place=MAIN):
                wait(pe, place[1], done)
                for b in range(CB):
                    ins = t.matmul(place[0][:, b * NE:(b + 1) * NE], x2tf[:, b * 128:(b + 1) * 128], gw_s[:, :],
                                   start=True, stop=True)
                ins.then_inc(s_gl, 1)

            def routing_transpose(c, done, place=MAIN):
                wait(pe, s_rw, c + 1)
                wait(pe, place[1], done)
                for b in range(CB):
                    ins = t.transpose(place[0][:, 64 * b:64 * b + 64].bitcast(F16),
                                      rwcat[:, b, :, :].rearrange("p k e -> p (k e)"), ident_h[:, :])
                ins.then_inc(s_rwt, 1)

            pe.wait_ge(s_cst, 16)
            ctx_transpose(0, 0, head("ct"))
            x_transpose(0, 0, head("xt"))
            pe.wait_ge(s_proj, 16 * 5)
            project(wk_s, cnt, after("head", "ct"), s_kp, head("k"))
            project(wq_s, xnt, after("head", "xt"), s_qp, head("q"))
            project_v(after("head", "ct"), head("v"))
            pe.wait_ge(s_sel, 16)
            pe.wait_ge(s_prep, 10)
            select_k(0, 0, 0)
            select_q(0, 0, 0, head("selq0"))
            select_q(0, 1, after("head", "ct"), head("selq1"))
            pe.wait_ge(s_b6, after("head", "selq1"))
            pe.wait_ge(s_const, 16 * 5)
            scores(0, 0)

            def first_slot(c):
                key_scores(c, 0)
                max_transpose(c, 0)
                scores(c, 1)

            first_slot(0)

            def chunk(c, prev, nxt):
                def at(use):
                    return before(c, use)

                for u in range(NU):
                    b = u // 2
                    if u:
                        key_scores(c, u)
                        max_transpose(c, u)

                    if 0 < u < NU - 1:
                        scores(c, u + 1)
                    elif u and nxt:
                        scores(c + 1, 0)

                    if u == 1 and prev:
                        out_transpose(c - 1, CB - 1, at("ot3"))
                    if u == 2 and nxt:
                        x_transpose(c + 1, at("xt"))
                    if u == 3 and prev:
                        x2_transpose(c - 1, at("x2t"))
                    if u in (4, 6, 7):
                        out_transpose(c, u // 2 - 2 + u % 2, at(f"ot{u // 2 - 2 + u % 2}"))
                    mask_and_max(c, u)

                    if u == 1 and prev:
                        attention_out(at("wo"))
                    if u == 2 and nxt:
                        ctx_transpose(c + 1, at("ct"))
                    if u == 3 and prev:
                        gate(at("gate"))
                    if u == 5 and nxt:
                        select_q(c + 1, 0, at("selq0"))
                    if u == 7 and nxt:
                        project_v(at("v"))

                    if u:
                        attend(c, u - 1)
                    elif prev:
                        attend(c - 1, NU - 1)

                    if u in (0, 2, 4):
                        select_k(c, b + 1, NU * c + u + 2)
                    if u == 6 and nxt:
                        select_k(c + 1, 0, NU * c + u + 2)
                    if u in (0, 2):
                        select_q(c, b + 2, at(f"selq{b + 2}"))
                    elif u == 6 and nxt:
                        select_q(c + 1, 1, at("selq1"))
                    if u == 3 and nxt:
                        project(wq_s, xnt, at("q"), s_qp)
                    if u == 5 and nxt:
                        project(wk_s, cnt, at("k"), s_kp)
                    if u == 7 and nxt:
                        first_slot(c + 1)
                    if u == 7 and prev:
                        routing_transpose(c - 1, at("rwt"))

            chunk(0, False, True)
            with pe.Fori(1, NC - 1) as c:
                chunk(c, True, True)
            chunk(NC - 1, True, False)
            attend(NC - 1, NU - 1)

            pe.wait_ge(s_exp, NC * NU)
            pe.wait_ge(s_b6, after(NC - 1, "rwt"))
            pe.wait_ge(s_x2l, NC - 1)
            pe.wait_ge(s_wsplit, NP)
            pe.wait_ge(s_oh, 16)

            def split_product(out, w_at, a, b, start, stop):
                t.matmul(out, w_hi[:, w_at], a, start=start, stop=False)
                t.matmul(out, w_hi[:, w_at], b, start=False, stop=False)
                return t.matmul(out, w_lo[:, w_at], a, start=False, stop=stop)

            def gate_and_up(n, c, k, block):
                wait(pe, s_sg, n - 1)
                wait(pe, s_gup, n - 1)
                tok = bass.ds(c * CT, CT)
                a, b = x2t_hi[:, tok], x2t_lo[:, tok]
                split_product(bank(k % 2), bass.ds(block * 128, 128), a, b, True, True).then_inc(s_g, 1)
                split_product(bank(2 + k % 2), bass.ds(WC + block * 128, 128), a, b, True, True).then_inc(s_u, 1)

            def expand(n, c, k, block):
                wait(pe, s_h, n - 1)
                t.matmul(bank(4 + k % 2), onehot_s[:, bass.ds(block * 128, 128)], rwt[:, bass.ds(c * CT, CT)],
                         start=True, stop=True).then_inc(s_rwe, 1)

            def down(n, k, block, start=False, stop=False):
                wait(pe, s_hl, n + 1)
                split_product(bank(6), bass.ds(2 * WC + block * 128, 128), h_hi[:, k % 2, :], h_lo[:, k % 2, :],
                              start, stop).then_inc(s_d, 1)

            def y_transpose(c):
                wait(pe, s_yc, c + 1)
                wait(pe, s_fin, c)
                for b in range(CB):
                    ins = t.transpose(bank(7)[:, b * 128:(b + 1) * 128], y_s[:, b * 128:(b + 1) * 128], ident)
                ins.then_inc(s_yt, 1)

            def first_turn(c, k):
                n = c * RB
                gate_and_up(n + RS + k, c, k, k)
                expand(n + RS + k, c, k, k)
                if k == 0:
                    wait(pe, s_yc, c)
                down(n + k, k, RR + k if k < RS else k - RS, start=k == 0)

            def turns(c):
                n = c * RB
                with pe.Fori(1, RR // RU) as turn:
                    r = turn * RU
                    for k in range(RU):
                        gate_and_up(n + r + (RS + k), c, k, r + k)
                        expand(n + r + (RS + k), c, k, r + k)
                        down(n + r + k, k, r + (k - RS))

            gate_and_up(0, 0, 0, RR)
            out_transpose(NC - 1, CB - 1, tail("ot3"), TAIL)
            gate_and_up(1, 0, 1, RR + 1)
            attention_out(tail("wo"), TAIL)
            for k in range(RU):
                first_turn(0, k)
                if k == 2:
                    x2_transpose(NC - 1, tail("x2t"), TAIL)
                if k == 3:
                    gate(tail("gate"), TAIL)
            turns(0)
            routing_transpose(NC - 1, tail("rwt"), TAIL)
            pe.wait_ge(s_x2l, NC)
            pe.wait_ge(s_b7, tail("rwt") + 1)

            with pe.Fori(1, NC) as c:
                for k in range(RS):
                    gate_and_up(c * RB + k, c, k, RR + k)
                    down(c * RB + k - 2, k, RR - 2 + k, stop=k == 1)
                for k in range(RU):
                    first_turn(c, k)
                turns(c)
                y_transpose(c - 1)

            for k in range(2):
                down(NC * RB - 2 + k, k, RR - 2 + k, stop=k == 1)
            y_transpose(NC - 1)


def kernel(x, ctx_1024, mask_BxSxS2_ik1, L0_xattn_Wq, L0_xattn_bq, L0_xattn_Wk, L0_xattn_bk, L0_xattn_Wv,
           L0_xattn_bv, L0_xattn_Wo, L0_xattn_bo, L0_ffn_gate_w, L0_ffn_gate_bias, L0_ffn_Wg, L0_ffn_Wu,
           L0_ffn_Wd, L0_ffn_Sg, L0_ffn_Su, L0_ffn_Sd):
    import concourse.bacc as bacc
    from concourse.bass_utils import run_bass_kernel_spmd

    a = np.ascontiguousarray
    pad = np.zeros((WC - NE * EI - SI, D), np.float32)
    rows_g = np.concatenate([np.asarray(L0_ffn_Wg).reshape(NE * EI, D), np.asarray(L0_ffn_Sg), pad])
    rows_u = np.concatenate([np.asarray(L0_ffn_Wu).reshape(NE * EI, D), np.asarray(L0_ffn_Su), pad])
    rows_d = np.concatenate([np.asarray(L0_ffn_Wd).transpose(0, 2, 1).reshape(NE * EI, D), np.asarray(L0_ffn_Sd).T, pad])
    w_all = np.concatenate([rows_g.T, rows_u.T, rows_d.reshape(RB, 128, D).transpose(1, 0, 2).reshape(128, RB * D)], 1)

    p = np.arange(128)[:, None]
    g = np.arange(HQ)[None, :]
    own, other = np.divmod(np.arange(NG * NG)[None, :], NG)
    consts = np.concatenate([np.eye(128), (p % 32) // DK == g, p % 32 == g, np.broadcast_to(other < own, (128, NG * NG))],
                            1).astype(np.float32)
    part, row, j, col = np.ogrid[0:4, 0:128, 0:4, 0:128]
    takes = np.array([[1, 0, 1, 0], [0, 1, 0, 0], [1, 1, 0, 0], [0, 0, 1, 0]])
    sel = ((row == 32 * j + col % 32) & (takes[part, col // 32] == 1)).transpose(1, 0, 2, 3).astype(np.float16)
    onehot = (p % NE == np.arange(RR * 128)[None, :] // EI).astype(np.float16)

    arrays = {
        "x": np.asarray(x), "ctx": np.asarray(ctx_1024), "mask": np.asarray(mask_BxSxS2_ik1),
        "wq": np.asarray(L0_xattn_Wq).T, "wk": np.asarray(L0_xattn_Wk).T,
        "wv": np.asarray(L0_xattn_Wv).T, "wo": np.asarray(L0_xattn_Wo).T,
        "bq": np.asarray(L0_xattn_bq).reshape(D, 1), "bk": np.asarray(L0_xattn_bk).reshape(D, 1),
        "bv": np.asarray(L0_xattn_bv), "bo": np.asarray(L0_xattn_bo),
        "gate_w": np.asarray(L0_ffn_gate_w).T, "gate_b": np.asarray(L0_ffn_gate_bias),
        "w_all": w_all, "consts": consts, "sel": sel, "onehot": onehot,
    }
    arrays = {k + "_dram": a(v) for k, v in arrays.items()}
    nc = bacc.Bacc("TRN2", target_bir_lowering=False, num_devices=1)
    args = [nc.dram_tensor(k, v.shape, mybir.dt.from_np(v.dtype), kind="ExternalInput").ap() for k, v in arrays.items()]
    args.append(nc.dram_tensor("out_dram", (B, T, D), F32, kind="ExternalOutput").ap())
    build(nc, *args)
    r = run_bass_kernel_spmd(nc, [arrays], core_ids=[0])
    return r.results[0]["out_dram"]
```
